# Optimizing a Trainium2 kernel written in Bass

```python
import numpy as np
import jax
import jax.numpy as jnp

def _softmax(x, axis=-1):
    return jax.nn.softmax(x, axis=axis)

def _gelu(x):
    return jax.nn.gelu(x, approximate=True)

def _silu(x):
    return jax.nn.silu(x)

def _sigmoid(x):
    return jax.nn.sigmoid(x)

def _layernorm(x, axis=-1, eps=1e-05):
    m = jnp.mean(x, axis=axis, keepdims=True)
    v = jnp.var(x, axis=axis, keepdims=True)
    return (x - m) / jnp.sqrt(v + eps)

def _scatter_add(tgt, idx, src, axis=0):
    return tgt.at[idx].add(src)

def _segment_sum(src, seg, n):
    return jax.ops.segment_sum(src, seg, n)
kernel_name = 'mk_seq_preln_d2_jaxref_r8_fc0cfc'

def setup_inputs(seed: int=0):
    np.random.seed(seed)
    _w = jnp.asarray

    def _L0_attn_setup():
        import jax, jax.numpy as jnp
        import numpy as np
        import math
        RIEMANN_ZEROS_IM = (14.134725142, 21.022039639, 25.01085758, 30.424876126, 32.935061588, 37.586178159, 40.918719012, 43.327073281, 48.005150881, 49.773832478, 52.970321478, 56.446247697, 59.347044003, 60.831778525, 65.112544048, 67.079810529, 69.546401711, 72.067157674, 75.704690699, 77.144840069, 79.33737502, 82.910380854, 84.735492981, 87.425274613, 88.809111208, 92.491899271, 94.651344041, 95.870634228, 98.831194218, 101.317851006, 103.72553804, 105.446623052)
        D_MODEL = 128
        N_HEADS = 16
        D_HEAD = D_MODEL // N_HEADS
        N_PAIRS = D_HEAD // 2
        _gamma = np.asarray(RIEMANN_ZEROS_IM[:N_PAIRS], dtype=np.float32)
        INV_FREQ = jnp.asarray(1.0 / (_gamma / _gamma[0]))

        def _rotate(x, cos, sin):
            x1 = x[..., 0::2]
            x2 = x[..., 1::2]
            rx1 = x1 * cos - x2 * sin
            rx2 = x1 * sin + x2 * cos
            return jnp.stack([rx1, rx2], axis=-1).reshape(x.shape)
        key = jax.random.key(seed)
        k1, k2, k3 = jax.random.split(key, 3)
        b, n = (4, 256)
        x = jax.random.normal(k1, (b, n, D_MODEL), dtype=jnp.float32)
        w_qkv = jax.random.normal(k2, (D_MODEL, 3 * D_MODEL), dtype=jnp.float32) / math.sqrt(D_MODEL)
        w_o = jax.random.normal(k3, (D_MODEL, D_MODEL), dtype=jnp.float32) / math.sqrt(D_MODEL)
        log_scale = jnp.zeros((N_HEADS,), dtype=jnp.float32)
        return {'x': x, 'w_qkv': w_qkv, 'w_o': w_o, 'log_scale': log_scale}
    _L0_attn_in = _L0_attn_setup()

    def _L0_ffn_setup():
        import jax, jax.numpy as jnp
        import numpy as np

        def _binarize(w):
            alpha = jax.lax.stop_gradient(jnp.mean(jnp.abs(w), axis=1, keepdims=True))
            bw = alpha * jnp.sign(w)
            return w + jax.lax.stop_gradient(bw - w)
        key = jax.random.key(seed)
        k1, k2, k3, k4, k5 = jax.random.split(key, 5)
        D, H = (128, 512)
        x = jax.random.normal(k1, (64, 196, D), dtype=jnp.float32)
        w1 = jax.random.normal(k2, (H, D), dtype=jnp.float32) * 0.02
        b1 = jax.random.normal(k3, (H,), dtype=jnp.float32) * 0.02
        w2 = jax.random.normal(k4, (D, H), dtype=jnp.float32) * 0.02
        b2 = jax.random.normal(k5, (D,), dtype=jnp.float32) * 0.02
        return {'x': x, 'w1': w1, 'b1': b1, 'w2': w2, 'b2': b2}
    _L0_ffn_in = _L0_ffn_setup()

    def _L1_attn_setup():
        import jax, jax.numpy as jnp
        import numpy as np
        B, T, D, H = (2, 256, 128, 16)
        DH = D // H
        ROPE_BASE = 10000.0

        def _rope(Xh, cos, sin):
            x0 = Xh[..., 0::2]
            x1 = Xh[..., 1::2]
            r0 = cos * x0 - sin * x1
            r1 = sin * x0 + cos * x1
            return jnp.stack((r0, r1), axis=-1).reshape(Xh.shape)
        key = jax.random.key(seed)
        ks = jax.random.split(key, 5)
        s = 1.0 / np.sqrt(D)
        return {'X': jax.random.normal(ks[0], (B, T, D), dtype=jnp.float32), 'W_q': jax.random.normal(ks[1], (D, D), dtype=jnp.float32) * s, 'W_k': jax.random.normal(ks[2], (D, D), dtype=jnp.float32) * s, 'W_v': jax.random.normal(ks[3], (D, D), dtype=jnp.float32) * s, 'W_o': jax.random.normal(ks[4], (D, D), dtype=jnp.float32) * s}
    _L1_attn_in = _L1_attn_setup()

    def _L1_ffn_setup():
        import jax, jax.numpy as jnp
        import numpy as np
        DIM = 128
        HIDDEN = 384
        SCALE = 1.0 / 127.0

        def _dequant(w_int, dtype):
            return w_int.astype(dtype) * jnp.asarray(SCALE, dtype)
        key = jax.random.key(seed)
        k_x, k_g, k_u, k_d = jax.random.split(key, 4)
        x = jax.random.normal(k_x, (4, 256, DIM), dtype=jnp.float32)
        w_gate = jax.random.randint(k_g, (HIDDEN, DIM), -127, 128, dtype=jnp.int32)
        w_up = jax.random.randint(k_u, (HIDDEN, DIM), -127, 128, dtype=jnp.int32)
        w_down = jax.random.randint(k_d, (DIM, HIDDEN), -127, 128, dtype=jnp.int32)
        return {'x': x, 'w_gate': w_gate, 'w_up': w_up, 'w_down': w_down}
    _L1_ffn_in = _L1_ffn_setup()
    _d = {'L0_attn_x': _L0_attn_in['x'], 'L0_attn_w_qkv': _L0_attn_in['w_qkv'], 'L0_attn_w_o': _L0_attn_in['w_o'], 'L0_attn_log_scale': _L0_attn_in['log_scale'], 'L0_ffn_w1': _L0_ffn_in['w1'], 'L0_ffn_b1': _L0_ffn_in['b1'], 'L0_ffn_w2': _L0_ffn_in['w2'], 'L0_ffn_b2': _L0_ffn_in['b2'], 'L1_attn_W_q': _L1_attn_in['W_q'], 'L1_attn_W_k': _L1_attn_in['W_k'], 'L1_attn_W_v': _L1_attn_in['W_v'], 'L1_attn_W_o': _L1_attn_in['W_o'], 'L1_ffn_w_gate': _L1_ffn_in['w_gate'], 'L1_ffn_w_up': _L1_ffn_in['w_up'], 'L1_ffn_w_down': _L1_ffn_in['w_down']}
    _x0 = _d['L0_attn_x']
    _d['L0_attn_x'] = jax.random.normal(jax.random.fold_in(jax.random.key(seed), 1), (1, 2048, 128), dtype=_x0.dtype)
    del _x0
    return _d

def reference(L0_attn_x, L0_attn_w_qkv, L0_attn_w_o, L0_attn_log_scale, L0_ffn_w1, L0_ffn_b1, L0_ffn_w2, L0_ffn_b2, L1_attn_W_q, L1_attn_W_k, L1_attn_W_v, L1_attn_W_o, L1_ffn_w_gate, L1_ffn_w_up, L1_ffn_w_down):

    def _L0_attn_ref(x, w_qkv, w_o, log_scale):
        import jax, jax.numpy as jnp
        import numpy as np
        import math
        RIEMANN_ZEROS_IM = (14.134725142, 21.022039639, 25.01085758, 30.424876126, 32.935061588, 37.586178159, 40.918719012, 43.327073281, 48.005150881, 49.773832478, 52.970321478, 56.446247697, 59.347044003, 60.831778525, 65.112544048, 67.079810529, 69.546401711, 72.067157674, 75.704690699, 77.144840069, 79.33737502, 82.910380854, 84.735492981, 87.425274613, 88.809111208, 92.491899271, 94.651344041, 95.870634228, 98.831194218, 101.317851006, 103.72553804, 105.446623052)
        D_MODEL = 128
        N_HEADS = 16
        D_HEAD = D_MODEL // N_HEADS
        N_PAIRS = D_HEAD // 2
        _gamma = np.asarray(RIEMANN_ZEROS_IM[:N_PAIRS], dtype=np.float32)
        INV_FREQ = jnp.asarray(1.0 / (_gamma / _gamma[0]))

        def _rotate(x, cos, sin):
            x1 = x[..., 0::2]
            x2 = x[..., 1::2]
            rx1 = x1 * cos - x2 * sin
            rx2 = x1 * sin + x2 * cos
            return jnp.stack([rx1, rx2], axis=-1).reshape(x.shape)
        b, n, d = x.shape
        qkv = (x @ w_qkv).reshape(b, n, 3, N_HEADS, D_HEAD)
        q, k, v = (qkv[:, :, 0], qkv[:, :, 1], qkv[:, :, 2])
        q = q.transpose(0, 2, 1, 3)
        k = k.transpose(0, 2, 1, 3)
        v = v.transpose(0, 2, 1, 3)
        scale = jnp.exp(log_scale)
        pos = jnp.arange(n, dtype=jnp.float32)
        theta = pos[None, None, :, None] * INV_FREQ[None, None, None, :] * scale[None, :, None, None]
        cos, sin = (jnp.cos(theta), jnp.sin(theta))
        q = _rotate(q, cos, sin)
        k = _rotate(k, cos, sin)
        scores = jnp.einsum('bhqd,bhkd->bhqk', q, k) / math.sqrt(D_HEAD)
        causal = jnp.tril(jnp.ones((n, n), dtype=bool))
        scores = jnp.where(causal[None, None], scores, -jnp.inf)
        attn = jax.nn.softmax(scores, axis=-1)
        out = jnp.einsum('bhqk,bhkd->bhqd', attn, v)
        out = out.transpose(0, 2, 1, 3).reshape(b, n, d)
        return out @ w_o

    def _L0_ffn_ref(x, w1, b1, w2, b2):
        import jax, jax.numpy as jnp
        import numpy as np

        def _binarize(w):
            alpha = jax.lax.stop_gradient(jnp.mean(jnp.abs(w), axis=1, keepdims=True))
            bw = alpha * jnp.sign(w)
            return w + jax.lax.stop_gradient(bw - w)
        bw1 = _binarize(w1)
        h = jnp.einsum('bsd,hd->bsh', x, bw1) + b1
        h = jax.nn.gelu(h, approximate=False)
        bw2 = _binarize(w2)
        out = jnp.einsum('bsh,dh->bsd', h, bw2) + b2
        return out

    def _L1_attn_ref(X, W_q, W_k, W_v, W_o):
        import jax, jax.numpy as jnp
        import numpy as np
        B, T, D, H = (2, 256, 128, 16)
        DH = D // H
        ROPE_BASE = 10000.0

        def _rope(Xh, cos, sin):
            x0 = Xh[..., 0::2]
            x1 = Xh[..., 1::2]
            r0 = cos * x0 - sin * x1
            r1 = sin * x0 + cos * x1
            return jnp.stack((r0, r1), axis=-1).reshape(Xh.shape)
        b, t, d = X.shape
        Q = X @ W_q.T
        K = X @ W_k.T
        V = X @ W_v.T
        Qh = Q.reshape(b, t, H, DH).transpose(0, 2, 1, 3)
        Kh = K.reshape(b, t, H, DH).transpose(0, 2, 1, 3)
        Vh = V.reshape(b, t, H, DH).transpose(0, 2, 1, 3)
        theta = ROPE_BASE ** (-2.0 * jnp.arange(DH // 2, dtype=jnp.float32) / DH)
        pos = jnp.arange(t, dtype=jnp.float32)
        angles = pos[:, None] * theta[None, :]
        cos = jnp.cos(angles).astype(Qh.dtype)
        sin = jnp.sin(angles).astype(Qh.dtype)
        Qr = _rope(Qh, cos, sin)
        Kr = _rope(Kh, cos, sin)
        scores = jnp.einsum('bhqd,bhkd->bhqk', Qr, Kr) * DH ** (-0.5)
        causal = jnp.triu(jnp.ones((t, t), dtype=bool), 1)
        neg = jnp.finfo(scores.dtype).min
        scores = jnp.where(causal[None, None], neg, scores)
        pattern = jax.nn.softmax(scores, axis=-1)
        heads = jnp.einsum('bhqk,bhkd->bhqd', pattern, Vh)
        out = heads.transpose(0, 2, 1, 3).reshape(b, t, d)
        return out @ W_o.T

    def _L1_ffn_ref(x, w_gate, w_up, w_down):
        import jax, jax.numpy as jnp
        import numpy as np
        DIM = 128
        HIDDEN = 384
        SCALE = 1.0 / 127.0

        def _dequant(w_int, dtype):
            return w_int.astype(dtype) * jnp.asarray(SCALE, dtype)
        wg = _dequant(w_gate, x.dtype)
        wu = _dequant(w_up, x.dtype)
        wd = _dequant(w_down, x.dtype)
        gate = jnp.einsum('bsd,hd->bsh', x, wg)
        up = jnp.einsum('bsd,hd->bsh', x, wu)
        h = jax.nn.silu(gate) * up
        return jnp.einsum('bsh,dh->bsd', h, wd)
    x = L0_attn_x
    x = x + _L0_attn_ref(_layernorm(x, axis=-1), L0_attn_w_qkv, L0_attn_w_o, L0_attn_log_scale)
    x = x + _L0_ffn_ref(_layernorm(x, axis=-1), L0_ffn_w1, L0_ffn_b1, L0_ffn_w2, L0_ffn_b2)
    x = x + _L1_attn_ref(_layernorm(x, axis=-1), L1_attn_W_q, L1_attn_W_k, L1_attn_W_v, L1_attn_W_o)
    x = x + _L1_ffn_ref(_layernorm(x, axis=-1), L1_ffn_w_gate, L1_ffn_w_up, L1_ffn_w_down)
    return x

_drawn_inputs = setup_inputs


def setup_inputs(seed=0):
    import zlib

    import numpy as np

    out = dict(_drawn_inputs(seed))
    spreads = {'L0_attn_log_scale': (0.0, 0.1)}
    factors = {'L0_ffn_b1': 7.148}
    for name, (base, spread) in spreads.items():
        noise = np.random.default_rng([zlib.crc32(name.encode()), seed]).standard_normal(out[name].shape)
        drawn = base * np.exp(spread * noise) if base else spread * noise
        out[name] = jnp.asarray(drawn.astype(out[name].dtype))
    for name, factor in factors.items():
        out[name] = (out[name] * factor).astype(out[name].dtype)
    return out
```

```python
from contextlib import ExitStack

import numpy as np

import concourse.bass as bass
from concourse import mybir

FP32, BF16, I32 = mybir.dt.float32, mybir.dt.bfloat16, mybir.dt.int32
ALU = mybir.AluOpType
ACT = mybir.ActivationFunctionType
AX = mybir.AxisListType

P = 128
T, D = 2048, 128
H, DH = 16, 8
NT = T // P
BLK = 512
TPB = BLK // P
NB = T // BLK
HG = 4
NG = H // HG
ROWS = 64
MROW = 48
VW = 32
HID0, HID1 = 512, 384
C0, C1 = HID0 // P, HID1 // P
EPS = 1e-5
SCALE = float(DH) ** -0.5
NEG = -1e30

FIRST = [sum(TPB * (q + 1) for q in range(b)) for b in range(NB + 1)]
STEPS = FIRST[NB]
LEAD = 20
NSLOT = 16
S_BANKS, E_BANKS, O_BANK, X_BANK = 0, 4, 6, 7


def block_of(step):
    return max(b for b in range(NB) if FIRST[b] <= step)


def rope_frequencies():
    gamma = np.asarray((14.134725142, 21.022039639, 25.01085758, 30.424876126), np.float32)
    inv0 = np.float32(1.0) / (gamma / gamma[0])
    inv1 = np.float32(10000.0) ** (np.float32(-2.0) * np.arange(DH // 2, dtype=np.float32) / np.float32(DH))
    return [float(v) for v in inv0], [float(v) for v in inv1.astype(np.float32)]


def wait(eng, sem, value):
    eng.wait_ge(sem, value)
    eng.sem_inc(wait.passed, 1)


class Chain:

    def __init__(self, eng, sem):
        self.eng, self.sem, self.n = eng, sem, 0

    def __call__(self, ins):
        self.n += 1
        ins.then_inc(self.sem, 1)
        self.eng.wait_ge(self.sem, self.n)

    def mark(self, ins):
        self.n += 1
        ins.then_inc(self.sem, 1)
        return self.n


def build(nc, x_in, w_qkv, w_o0, log_scale, w1, b1, w2, b2, w_q, w_k, w_v, w_o1, w_gate, w_up, w_down, out):
    ctx = ExitStack()
    with ctx:
        def sb(name, shape, dt):
            return ctx.enter_context(nc.sbuf_tensor(name, shape, dt))

        def sem(name):
            return ctx.enter_context(nc.semaphore(name))

        X = sb("x_res", [P, NT, D], FP32)
        XN = sb("x_norm", [P, NT, D], FP32)
        ATT = XN
        VX = sb("v_all", [P, NT, H, DH + 1], FP32)
        QA = sb("q_all", [P, H // 2, T], BF16)
        KA = sb("k_all", [P, H // 2, T], BF16)
        Q2 = sb("q_group", [P, HG // 2, T], BF16)
        K2 = sb("k_group", [P, HG, T], BF16)
        Q1 = sb("q_group_max", [P, T], BF16)
        K1 = sb("k_group_max", [P, T], BF16)
        VG = sb("v_group", [P, NT, HG, VW], FP32)
        WORK = sb("work", [P, 10240], FP32)
        SIN = sb("sin", [P, 2, NT, H * DH // 2], FP32)
        COS = sb("cos", [P, 2, NT, H * DH // 2], FP32)
        WQKV = sb("w_qkv_sb", [P, 2, 3 * D], FP32)
        WO = sb("w_o_sb", [P, 2, D], FP32)
        W1T = sb("w1_t", [P, HID0], FP32)
        W2T = sb("w2_t", [P, C0, D], FP32)
        WGT = sb("w_gate_t", [P, HID1], FP32)
        WUT = sb("w_up_t", [P, HID1], FP32)
        WDT = sb("w_down_t", [P, C1, D], FP32)
        B1 = sb("b1_sb", [P, C0], FP32)
        B2 = sb("b2_sb", [P, D], FP32)
        IDF = sb("ident_f", [P, P], FP32)
        IDB = sb("ident_b", [P, P], BF16)
        CM = sb("causal_b", [P, P], BF16)
        STAT = sb("ln_stat", [P, NT, 6], FP32)
        MV = sb("ln_mv", [P, NT, 2], FP32)
        VAR = sb("ln_var", [P, NT], FP32)
        ROOT = sb("ln_root", [P, NT], FP32)
        RSTD = sb("ln_rstd", [P, NT], FP32)
        MX = sb("max_parts", [P, NB, TPB, HG], FP32)
        NM = sb("neg_max", [P, TPB * HG], FP32)
        NR = sb("neg_max_rest", [P, 2, TPB * HG], FP32)
        MP = sb("neg_max_bf", [P, TPB, HG, 3], BF16)
        MT = sb("neg_max_rows", [HG * 3, BLK], BF16)
        OT = sb("o_rows", [P, BLK], FP32)
        RD = sb("o_recip", [P, TPB, HG], FP32)

        PS = ctx.enter_context(nc.psum_tensor("ps", [P, 8, 512], FP32))

        def bank(n):
            return PS[:, n, :]

        def bank_bf(n):
            return PS[:, n, :].bitcast(BF16)

        def work(at, n):
            return WORK[:, at:at + n]

        PR = WORK[:, 0:NSLOT * BLK].rearrange("p (s n) -> p s n", s=NSLOT)

        XNT = work(0, T)

        inv0, inv1 = rope_frequencies()

        ld_x = [sem(f"x_loaded{b}") for b in range(NB)]
        ld_w, ld_b = sem("weights_loaded"), sem("biases_loaded")
        ident_ready, pos_ready, scale_ready = sem("ident_ready"), sem("pos_ready"), sem("scale_ready")
        wait.passed = sem("waits_passed")
        pool_chain, dve_chain = sem("setup_pool_chain"), sem("setup_dve_chain")
        theta_ready, sin_ready, sq_ready = sem("theta_ready"), sem("sin_ready"), sem("sq_ready")
        raw_ready, w_turned, w_kept = sem("raw_ready"), sem("w_turned"), sem("w_kept")

        S1 = work(0, 512).rearrange("p (c n) -> p c n", c=C0)
        S2 = work(512, 512)
        SA = work(1024, 512).rearrange("p (c n) -> p c n", c=4)
        SI = [work(1536 + 384 * i, 384).bitcast(I32).rearrange("p (c n) -> p c n", c=C1) for i in range(3)]
        SF = [work(2688 + 384 * i, 384).rearrange("p (c n) -> p c n", c=C1) for i in range(3)]
        SG1, SG2 = work(3840, 512), work(4352, 512)
        TH = work(4864, 2048)
        KK = work(6912, 2048)
        POSI = work(8960, 16).bitcast(I32)
        POSF = work(8976, 16)
        TH0 = work(8992, 64).rearrange("p (i f) -> p i f", f=4)
        LSC = work(9056, 16)
        ESC = work(9072, 16)
        AL = work(9088, 8)

        with nc.Block() as block:
            @block.sync
            def _(sp):
                for b in range(NB):
                    sp.dma_start(X[:, TPB * b:TPB * (b + 1), :],
                                 x_in[0, BLK * b:BLK * (b + 1), :].rearrange("(i p) d -> p i d", p=P)).then_inc(ld_x[b], 16)
                sp.dma_start(S1, w1.rearrange("(c p) d -> p c d", p=P)).then_inc(ld_w, 16)
                sp.dma_start(S2, w2).then_inc(ld_w, 16)
                for n, w in enumerate((w_gate, w_up)):
                    sp.dma_start(SI[n], w.rearrange("(c p) d -> p c d", p=P)).then_inc(ld_w, 16)
                sp.dma_start(SI[2], w_down.rearrange("p (c n) -> p c n", c=C1)).then_inc(ld_w, 16)
                for n, w in enumerate((w_q, w_k, w_v, w_o1)):
                    sp.dma_start(SA[:, n, :], w).then_inc(ld_w, 16)
                sp.dma_start(WQKV[:, 0, :], w_qkv).then_inc(ld_w, 16)
                sp.dma_start(WO[:, 0, :], w_o0).then_inc(ld_w, 16)
                for b in range(NB):
                    sp.wait_ge(ld_x[b], 16)

            @block.gpsimd
            def _(pool):
                link = Chain(pool, pool_chain)
                pool.iota(POSI, pattern=[[P, NT]], base=0, channel_multiplier=1).then_inc(pos_ready, 1)
                pool.memset(IDF[:, :], 0.0).then_inc(pool_chain, 1)
                pool.memset(IDB[:, :], 0.0).then_inc(pool_chain, 1)
                pool.memset(CM[:, :], 0.0).then_inc(pool_chain, 1)
                pool.memset(VG[:, :, :, :], 0.0)
                pool.memset(K2[:, :, :], 0.0)
                pool.memset(VX[:, :, :, DH:DH + 1], 1.0)
                pool.wait_ge(pool_chain, 3)
                for m in (IDF, IDB):
                    pool.affine_select(out=m[:, :], in_=m[:, :], compare_op=ALU.not_equal, fill=1.0,
                                       base=0, pattern=[[-1, P]], channel_multiplier=1).then_inc(ident_ready, 1)
                pool.affine_select(out=CM[:, :], in_=CM[:, :], compare_op=ALU.is_ge, fill=NEG,
                                   base=0, pattern=[[-1, P]], channel_multiplier=1).then_inc(ident_ready, 1)

            @block.scalar
            def _(act):
                act.dma_start(LSC, log_scale.rearrange("(a n) -> a n", a=1).broadcast_to([P, H])).then_inc(ld_b, 16)
                act.dma_start(B1[:, :], b1.rearrange("(c p) -> p c", p=P), allow_slow_non_contiguous=True).then_inc(ld_b, 16)
                act.dma_start(B2[:, :], b2.rearrange("(a n) -> a n", a=1).broadcast_to([P, D])).then_inc(ld_b, 16)
                act.wait_ge(ld_b, 48)
                act.activation(ESC, LSC, ACT.Exp).then_inc(scale_ready, 1)
                act.wait_ge(theta_ready, 1)
                act.activation(SIN[:, :, :, :].rearrange("p l i m -> p (l i m)"), TH, ACT.Sin).then_inc(sin_ready, 1)
                act.activation(KK, TH, ACT.Sin, scale=0.5).then_inc(sin_ready, 1)
                for n, dst in enumerate((W1T[:, :], W2T[:, :, :].rearrange("p c n -> p (c n)"),
                                         None, WGT[:, :], WUT[:, :], WDT[:, :, :].rearrange("p c n -> p (c n)"))):
                    act.wait_ge(w_turned, n + 1)
                    if dst is None:
                        act.activation(WQKV[:, 1, :], PS[:, n, 0:3 * D], ACT.Copy).then_inc(w_kept, 1)
                        act.activation(WO[:, 1, :], PS[:, n, 3 * D:4 * D], ACT.Copy).then_inc(w_kept, 1)
                    else:
                        act.activation(dst, PS[:, n, 0:dst.shape[1]], ACT.Copy).then_inc(w_kept, 1)
                act.wait_ge(w_kept, 7)

            @block.vector
            def _(dve):
                link = Chain(dve, dve_chain)
                dve.wait_ge(pos_ready, 1)
                link(dve.tensor_copy(POSF, POSI))
                for layer, inv in enumerate((inv0, inv1)):
                    for f in range(DH // 2):
                        link(dve.tensor_scalar(TH0[:, :, f], POSF, inv[f], None, ALU.mult))
                    th = TH.rearrange("p (l i h f) -> p l i h f", l=2, i=NT, h=H)[:, layer]
                    t0 = TH0.unsqueeze(2).broadcast_to([P, NT, H, DH // 2])
                    if layer == 0:
                        dve.wait_ge(scale_ready, 1)
                        e = ESC.unsqueeze(1).unsqueeze(3).broadcast_to([P, NT, H, DH // 2])
                        link(dve.tensor_tensor(th, t0, e, ALU.mult))
                    else:
                        link(dve.tensor_copy(th, t0))
                magic = 1.5 * 2.0 ** 23
                parts = (6.28125, float(np.float32(2 * np.pi - 6.28125).astype(np.float32)), 0.0)
                c2 = float(np.float32(np.round((2 * np.pi - 6.28125) * 2 ** 21) / 2 ** 21))
                c3 = float(np.float32(2 * np.pi - 6.28125 - c2))
                link(dve.tensor_scalar(KK, TH, float(1 / (2 * np.pi)), magic, ALU.mult, ALU.add))
                link(dve.tensor_scalar(KK, KK, magic, None, ALU.subtract))
                for c in (parts[0], c2, c3):
                    link(dve.scalar_tensor_tensor(out=TH, in0=KK, scalar=-c, in1=TH, op0=ALU.mult, op1=ALU.add))
                dve.tensor_scalar(TH, TH, 3.1415925, -3.1415925, ALU.min, ALU.max).then_inc(theta_ready, 1)
                dve.wait_ge(ld_w, 16 * 11)
                for n, (s, red) in enumerate(((S1, P), (S2.unsqueeze(1), HID0))):
                    c = s.shape[1]
                    al = AL[:, 4 * n:4 * n + c]
                    g1 = SG1.rearrange("p (c n) -> p c n", c=c)
                    g2 = SG2.rearrange("p (c n) -> p c n", c=c)
                    link(dve.tensor_reduce(al, s, AX.X, ALU.add, apply_absolute_value=True))
                    link(dve.tensor_scalar(al, al, 1.0 / red, None, ALU.mult))
                    link(dve.tensor_scalar(g1, s, 0.0, None, ALU.is_gt))
                    link(dve.tensor_scalar(g2, s, 0.0, None, ALU.is_lt))
                    link(dve.tensor_tensor(g1, g1, g2, ALU.subtract))
                    link(dve.tensor_tensor(g1, g1, al.unsqueeze(2).broadcast_to([P, c, 512 // c]), ALU.mult))
                    link(dve.tensor_tensor(g1, g1, s, ALU.subtract))
                    link(dve.tensor_tensor(s, s, g1, ALU.add))
                for n in range(3):
                    link(dve.tensor_scalar(SF[n], SI[n], float(np.float32(1.0 / 127.0)), None, ALU.mult))
                dve.sem_inc(raw_ready, 1)
                dve.wait_ge(sin_ready, 2)
                link(dve.tensor_tensor(KK, KK, KK, ALU.mult))
                link(dve.tensor_scalar(COS[:, :, :, :].rearrange("p l i m -> p (l i m)"), KK, -2.0, 1.0,
                                       ALU.mult, ALU.add))

            @block.tensor
            def _(pe):
                pe.wait_ge(ident_ready, 3)
                pe.wait_ge(raw_ready, 1)
                groups = [[S1[:, c, :] for c in range(C0)], [S2[:, c * P:(c + 1) * P] for c in range(C0)],
                          [SA[:, n, :] for n in range(4)]] + [[SF[n][:, c, :] for c in range(C1)] for n in range(3)]
                for n, group in enumerate(groups):
                    for c, src in enumerate(group):
                        last = pe.transpose(PS[:, n, c * P:(c + 1) * P], src, IDF[:, :])
                    last.then_inc(w_turned, 1)

        def row_statistics(dve, link, b, var_ready):
            ts = slice(TPB * b, TPB * (b + 1))
            for i in range(TPB * b, TPB * (b + 1)):
                n = link.mark(dve.bn_stats(STAT[:, i, :], X[:, i, :]))
            for i in range(TPB * b, TPB * (b + 1)):
                dve.wait_ge(link.sem, n)
                m = link.mark(dve.bn_aggr(MV[:, i, :], STAT[:, i, :]))
            dve.wait_ge(link.sem, m)
            dve.tensor_scalar(VAR[:, ts], MV[:, ts, 1], EPS, None, ALU.add).then_inc(var_ready, 1)

        def root(act, b, var_ready, root_ready):
            ts = slice(TPB * b, TPB * (b + 1))
            act.wait_ge(var_ready, b + 1)
            act.activation(ROOT[:, ts], VAR[:, ts], ACT.Sqrt).then_inc(root_ready, 1)

        def normalise_rows(dve, link, b, root_ready):
            ts = slice(TPB * b, TPB * (b + 1))
            dve.wait_ge(root_ready, b + 1)
            link(dve.reciprocal(RSTD[:, ts], ROOT[:, ts]))
            link(dve.tensor_tensor(ROOT[:, ts], RSTD[:, ts], RSTD[:, ts], ALU.mult))
            link(dve.tensor_tensor(ROOT[:, ts], ROOT[:, ts], VAR[:, ts], ALU.mult))
            link(dve.tensor_scalar(ROOT[:, ts], ROOT[:, ts], -0.5, 1.5, ALU.mult, ALU.add))
            link(dve.tensor_tensor(RSTD[:, ts], RSTD[:, ts], ROOT[:, ts], ALU.mult))
            for i in range(TPB * b, TPB * (b + 1)):
                last = dve.tensor_scalar(XN[:, i, :], X[:, i, :], MV[:, i, 0:1], RSTD[:, i:i + 1],
                                         ALU.subtract, ALU.mult)
            return last

        def attention_operands(layer):
            L = f"l{layer}_"
            normed, turned, kept = sem(L + "normed"), sem(L + "xn_turned"), sem(L + "xn_kept")
            qkv_ready, qk_kept, v_kept = sem(L + "qkv_ready"), sem(L + "qk_kept"), sem(L + "v_kept")
            chain, rotated, rest1, rest2 = sem(L + "op_chain"), sem(L + "rotated"), sem(L + "rest1"), sem(L + "rest2")
            high, mid, low, doubled = sem(L + "high"), sem(L + "mid"), sem(L + "low"), sem(L + "doubled")
            edge, stacked = sem(L + "edge"), sem(L + "stacked")
            var_ready, root_ready = sem(L + "var"), sem(L + "root")
            stored = [sem(L + "stored_act"), sem(L + "stored_dve")]

            QK = work(2048, 1024).rearrange("p (t a n) -> p t a n", t=TPB, a=2)
            ROT = work(3072, 1024).rearrange("p (t a n) -> p t a n", t=TPB, a=2)
            R1 = work(4096, 1024)
            R2 = work(5120, 1024)
            tmp = [work(4096 + 512 * n, 512).rearrange("p (t a m) -> p t a m", t=TPB, a=2) for n in range(4)]
            ASM = work(6144, 4096).bitcast(BF16).rearrange("p (t a h c) -> p t a h c", t=TPB, a=2, h=H)

            def rows(v):
                return v.rearrange("p (r d) -> p r d", d=DH)

            ROTf = rows(ROT.rearrange("p t a n -> p (t a n)"))
            ASMf = ASM.rearrange("p t a h c -> p (t a h) c")

            def part(a, n):
                return ASM[:, :, a, :, DH * n:DH * (n + 1)]

            with nc.Block() as block:
                def store(copy, b, f):
                    dst = (QA, KA)[f // 4][:, 2 * (f % 4):2 * (f % 4) + 2, BLK * b:BLK * (b + 1)]
                    return copy(dst, bank_bf(E_BANKS + f % 2).rearrange("p (s n) -> p s n", s=2))

                @block.vector
                def _(dve):
                    link = Chain(dve, chain)
                    for b in range(NB):
                        row_statistics(dve, link, b, var_ready)
                    for b in range(NB):
                        normalise_rows(dve, link, b, root_ready).then_inc(normed, 1)
                    for b in range(NB):
                        dve.wait_ge(qk_kept, b + 1)
                        x1, x2 = (QK.rearrange("p t a (m two) -> p t a m two", two=2)[:, :, :, :, n] for n in (0, 1))
                        y1, y2 = (ROT.rearrange("p t a (m two) -> p t a m two", two=2)[:, :, :, :, n] for n in (0, 1))
                        cos, sin = (v[:, layer, TPB * b:TPB * (b + 1), :].unsqueeze(2).broadcast_to([P, TPB, 2, D // 2])
                                    for v in (COS, SIN))
                        if b >= 1:
                            dve.wait_ge(low, b)
                        dve.tensor_tensor(tmp[0], x1, cos, ALU.mult)
                        dve.tensor_tensor(tmp[1], x2, sin, ALU.mult)
                        dve.tensor_tensor(tmp[2], x1, sin, ALU.mult)
                        link(dve.tensor_tensor(tmp[3], x2, cos, ALU.mult))
                        dve.tensor_tensor(y1, tmp[0], tmp[1], ALU.subtract)
                        dve.tensor_tensor(y2, tmp[2], tmp[3], ALU.add).then_inc(rotated, 1)
                        dve.wait_ge(high, b + 1)
                        dve.tensor_tensor(rows(R1), ROTf, ASMf[:, :, 0:DH], ALU.subtract).then_inc(rest1, 1)
                        dve.wait_ge(mid, b + 1)
                        dve.tensor_tensor(rows(R2), rows(R1), ASMf[:, :, 3 * DH:4 * DH], ALU.subtract).then_inc(rest2, 1)
                        for f in range(1, 8, 2):
                            dve.wait_ge(stacked, 8 * b + f + 1)
                            store(dve.tensor_copy, b, f).then_inc(stored[1], 1)

                @block.scalar
                def _(act):
                    for b in range(NB):
                        root(act, b, var_ready, root_ready)
                    for b in range(NB):
                        act.wait_ge(turned, b + 1)
                        act.activation(XNT[:, BLK * b:BLK * (b + 1)], bank(O_BANK + b % 2), ACT.Copy).then_inc(kept, 1)
                    for b in range(NB):
                        act.wait_ge(qkv_ready, b + 1)
                        if b >= 1:
                            act.wait_ge(rotated, b)
                        act.activation(QK.rearrange("p t a n -> p t (a n)"), PS[:, 0:TPB, 0:2 * D], ACT.Copy)\
                           .then_inc(qk_kept, 1)
                        act.activation(VX[:, TPB * b:TPB * (b + 1), :, 0:DH],
                                       PS[:, 0:TPB, 2 * D:3 * D].rearrange("p t (h d) -> p t h d", d=DH), ACT.Copy)\
                           .then_inc(v_kept, 1)
                        act.wait_ge(rotated, b + 1)
                        if b >= 1:
                            act.wait_ge(stacked, 8 * b)
                        act.activation(ASMf[:, :, 0:DH], ROTf, ACT.Copy).then_inc(high, 1)
                        act.wait_ge(rest1, b + 1)
                        act.activation(ASMf[:, :, 3 * DH:4 * DH], rows(R1), ACT.Copy).then_inc(mid, 1)
                        act.wait_ge(rest2, b + 1)
                        r2 = R2.rearrange("p (t a h d) -> p t a h d", t=TPB, a=2, h=H)
                        act.activation(part(0, 5), r2[:, :, 0], ACT.Copy)
                        act.activation(part(1, 4), r2[:, :, 1], ACT.Copy).then_inc(low, 1)
                        for f in range(0, 8, 2):
                            act.wait_ge(stacked, 8 * b + f + 1)
                            store(lambda o, i: act.activation(o, i, ACT.Copy), b, f).then_inc(stored[0], 1)

                @block.gpsimd
                def _(pool):
                    pool.memset(ASM[:, :, :, :, MROW:ROWS], 0.0).then_inc(edge, 1)
                    pool.wait_ge(edge, 1)
                    pool.memset(ASM[:, :, 1, :, MROW:MROW + 3], 1.0).then_inc(edge, 1)
                    for b in range(NB):
                        pool.wait_ge(high, b + 1)
                        pool.tensor_copy(part(0, 1), part(0, 0))
                        pool.tensor_copy(part(0, 4), part(0, 0))
                        pool.tensor_copy(part(1, 2), part(1, 0))
                        pool.tensor_copy(part(1, 5), part(1, 0))
                        pool.wait_ge(mid, b + 1)
                        pool.tensor_copy(part(0, 2), part(0, 3))
                        pool.tensor_copy(part(1, 1), part(1, 3)).then_inc(doubled, 1)

                @block.tensor
                def _(pe):
                    def turn(b):
                        pe.wait_ge(normed, b + 1)
                        if b >= 2:
                            pe.wait_ge(kept, b - 1)
                        for t in range(TPB):
                            last = pe.transpose(PS[:, O_BANK + b % 2, t * P:(t + 1) * P], XN[:, TPB * b + t, :], IDF[:, :])
                        last.then_inc(turned, 1)

                    def project(b):
                        pe.wait_ge(kept, b + 1)
                        if b >= 1:
                            pe.wait_ge(v_kept, b)
                        for t in range(TPB):
                            at = P * (TPB * b + t)
                            last = pe.matmul(PS[:, t, 0:3 * D], XNT[:, at:at + P], WQKV[:, layer, :], start=True, stop=True)
                        last.then_inc(qkv_ready, 1)

                    for b in range(NB):
                        turn(b)
                    project(0)
                    for b in range(NB):
                        if b + 1 < NB:
                            project(b + 1)
                        pe.wait_ge(low, b + 1)
                        pe.wait_ge(doubled, b + 1)
                        pe.wait_ge(edge, 2)
                        for f in range(8):
                            n = 4 * b + f // 2
                            if n >= 1:
                                pe.wait_ge(stored[f % 2], n)
                            for s in range(2):
                                for t in range(TPB):
                                    h = 2 * (2 * (f % 4) + s)
                                    last = pe.transpose(
                                        bank_bf(E_BANKS + f % 2)[:, s * BLK + t * P:s * BLK + (t + 1) * P],
                                        ASM[:, t, f // 4, h:h + 2, :].rearrange("p h c -> p (h c)"), IDB[:, :])
                            last.then_inc(stacked, 1)

        def attention(layer):
            L = f"l{layer}_"
            p1_loaded = [sem(f"{L}max_operands{b}") for b in range(NB)]
            p2_loaded = [sem(f"{L}operands{b}") for b in range(NB)]
            m_written = [sem(f"{L}max_rows{b}") for b in range(NB)]
            v_loaded = sem(L + "v_group")
            s_full, s_read = sem(L + "scores_full"), sem(L + "scores_read")
            nm_ready, nm_chain, mp_ready = sem(L + "neg_max"), sem(L + "split_chain"), sem(L + "max_split")
            m_turned, m_kept = sem(L + "max_turned"), sem(L + "max_kept")
            e_full, e_done, masked = sem(L + "exp_in"), sem(L + "exp_done"), sem(L + "masked")
            pv_done, o_kept, o_turned = sem(L + "pv_done"), sem(L + "o_kept"), sem(L + "o_turned")
            recip, normalised = sem(L + "recip"), sem(L + "normalised")

            from_one = {"scalar": (e_done, o_kept), "tensor": (pv_done, o_turned), "vector": (normalised,)}

            def max_step(t):
                b = block_of(t)
                c, q = divmod(t - FIRST[b], TPB)
                return b, c, q, (BLK if c < b else P * (q + 1))

            def exp_step(s):
                b = block_of(s)
                kt = s - FIRST[b]
                return b, kt, P * max(0, kt - TPB * b)

            def lead_of(g, s):
                t = s + LEAD
                return (g, t) if t < STEPS else (g + 1, t - STEPS)

            M_AT = {(FIRST[b + 1] - 1 - LEAD) % STEPS: b for b in range(NB)}
            O_AT = {FIRST[b + 1] + 2: b for b in range(NB - 1)}

            with nc.Block() as block:
                @block.sync
                def _(sp):
                    def load_max(g, b):
                        cols = slice(BLK * b, BLK * (b + 1))
                        for j in range(HG):
                            rows = slice(ROWS * (j % 2), ROWS * (j % 2) + 32)
                            for dst, src in ((Q1, QA), (K1, KA)):
                                sp.dma_start(dst[32 * j:32 * j + 32, cols],
                                             src[rows, bass.ds(g * 2 + j // 2, 1), cols].squeeze(1))\
                                  .then_inc(p1_loaded[b], 16)

                    def load_exp(g, b):
                        cols = slice(BLK * b, BLK * (b + 1))
                        for j in range(2):
                            rows = slice(ROWS * j, ROWS * (j + 1))
                            sp.dma_start(K2[rows, j:HG:2, cols], KA[rows, bass.ds(g * 2, 2), cols]).then_inc(p2_loaded[b], 16)
                        sp.dma_start(Q2[:, :, cols], QA[:, bass.ds(g * 2, 2), cols]).then_inc(p2_loaded[b], 16)

                    def write_max(g, b):
                        wait(sp, m_kept, g * NB + (b + 1))
                        wait(sp, p2_loaded[b], g * 48 + 48)
                        for j in range(HG):
                            at = ROWS * (j % 2) + MROW
                            sp.dma_start(Q2[at:at + 3, j // 2, BLK * b:BLK * (b + 1)], MT[3 * j:3 * j + 3, :])\
                              .then_inc(m_written[b], 16)

                    for b in range(NB):
                        load_max(0, b)
                        load_exp(0, b)
                    write_max(0, 0)
                    write_max(0, 1)
                    with sp.Fori(0, NG) as g:
                        nxt = (g + 1) & (NG - 1)
                        write_max(g, 2)
                        for b in range(NB):
                            wait(sp, s_full, g * (2 * STEPS) + 2 * (FIRST[NB - 1] + TPB * (b + 1)))
                            load_max(nxt, b)
                        write_max(g, 3)
                        for b in range(NB):
                            wait(sp, pv_done, g * STEPS + (FIRST[NB - 1] + TPB * (b + 1)) + 1)
                            load_exp(nxt, b)
                            if b < 2:
                                write_max(g + 1, b)
                    for b in range(NB):
                        sp.wait_ge(p1_loaded[b], 128 * (NG + 1))
                        sp.wait_ge(p2_loaded[b], 48 * (NG + 1))
                        sp.wait_ge(m_written[b], 64 * (NG + (b < 2)))

                @block.tensor
                def _(pe):
                    def maxima(g, t):
                        b, c, q, w = max_step(t)
                        if t == FIRST[b]:
                            pe.wait_ge(p1_loaded[b], g * 128 + 128)
                        at = P * (TPB * b + q)
                        for pair in range(2):
                            n = 2 * t + pair
                            if n >= 2 or not isinstance(g, int):
                                pe.wait_ge(s_read, g * (2 * STEPS) + (n - 1))
                            for j in (2 * pair, 2 * pair + 1):
                                rows = slice(32 * j, 32 * j + 32)
                                last = pe.matmul(PS[:, S_BANKS + j, 0:w], Q1[rows, at:at + P],
                                                 K1[rows, BLK * c:BLK * c + w], start=True, stop=(c < b))
                            if c == b:
                                for j in (2 * pair, 2 * pair + 1):
                                    last = pe.matmul(PS[:, S_BANKS + j, w - P:w], IDB[:, :], CM[:, :],
                                                     start=False, stop=True)
                            last.then_inc(s_full, 1)

                    def turn_max(g, b):
                        pe.wait_ge(mp_ready, g * NB + (b + 1))
                        n = g * NB + b
                        if not (isinstance(g, int) and n == 0):
                            pe.wait_ge(m_kept, n)
                        if not isinstance(g, int):
                            pe.wait_ge(normalised, outputs_before(g, b) + 1)
                        for q in range(TPB):
                            last = pe.transpose(bank_bf(X_BANK)[0:3 * HG, q * P:(q + 1) * P],
                                                MP[:, q, :, :].rearrange("p j n -> p (j n)"), IDB[:, :])
                        last.then_inc(m_turned, 1)

                    def outputs_before(g, b):
                        at = (FIRST[b + 1] - LEAD) % STEPS
                        before = sum(1 for s in O_AT if s < at)
                        return g * NB + before if b >= 2 else g * NB + (before - NB)

                    def maxima_before(s):
                        return 2 + sum(1 for m in M_AT if m + 1 < s)

                    def scores(g, s, j):
                        b, kt, q0 = exp_step(s)
                        if kt == 0 and j == 0:
                            pe.wait_ge(p2_loaded[b], g * 48 + 48)
                            pe.wait_ge(m_written[b], g * 64 + 64)
                        e = 4 * s + j
                        pe.wait_ge(e_done, g * (4 * STEPS) + max(0, e - 1) + 1)
                        pe.matmul(PS[:, E_BANKS + e % 2, 0:BLK - q0], K2[:, j, kt * P:(kt + 1) * P],
                                  Q2[:, j // 2, BLK * b + q0:BLK * (b + 1)], start=True, stop=True).then_inc(e_full, 1)

                    def product(g, s):
                        b, kt, q0 = exp_step(s)
                        if kt == 0:
                            pe.wait_ge(o_kept, g * NB + b + 1)
                            if b == 0:
                                pe.wait_ge(v_loaded, g * NB + NB)
                        pe.wait_ge(e_done, g * (4 * STEPS) + 4 * (s + 1) + 1)
                        if kt >= TPB * b:
                            pe.wait_ge(masked, g * NT + (kt + 1))
                        for j in range(HG):
                            last = pe.matmul(PS[VW * j:VW * (j + 1), O_BANK, q0:BLK], VG[:, kt, j, :],
                                             PR[:, (4 * s + j) % NSLOT, 0:BLK - q0],
                                             start=(kt == 0), stop=(kt == TPB * (b + 1) - 1))
                        last.then_inc(pv_done, 1)

                    def turn_output(g, b, s):
                        pe.wait_ge(o_kept, g * NB + (b + 1) + 1)
                        pe.wait_ge(m_kept, g * NB + maxima_before(s))
                        if b >= 1:
                            pe.wait_ge(normalised, g * NB + b + 1)
                        for q in range(TPB):
                            last = pe.transpose(PS[:, X_BANK, q * P:(q + 1) * P], OT[:, q * P:(q + 1) * P], IDF[:, :])
                        last.then_inc(o_turned, 1)

                    for t in range(LEAD):
                        maxima(0, t)
                        if (t + STEPS - LEAD - 1) % STEPS in M_AT and t >= 1:
                            turn_max(0, M_AT[(t + STEPS - LEAD - 1) % STEPS])
                    for s in from_one["tensor"]:
                        pe.sem_inc(s, 1)
                    with pe.Fori(0, NG) as g:
                        for s in range(STEPS):
                            scores(g, s, 0)
                            scores(g, s, 1)
                            if s >= 1:
                                product(g, s - 1)
                            scores(g, s, 2)
                            scores(g, s, 3)
                            if s == STEPS - 1:
                                product(g, s)
                            maxima(*lead_of(g, s))
                            if s - 1 in M_AT:
                                b = M_AT[s - 1]
                                turn_max(g if b >= 2 else g + 1, b)
                            if s in O_AT:
                                turn_output(g, O_AT[s], s)
                        turn_output(g, NB - 1, STEPS)

                @block.vector
                def _(dve):
                    def reduce(g, t):
                        b, c, q, w = max_step(t)
                        if t == FIRST[b] and not (isinstance(g, int) and t == 0):
                            dve.wait_ge(nm_ready, g * NB + b)
                        for pair in range(2):
                            dve.wait_ge(s_full, g * (2 * STEPS) + (2 * t + pair + 1))
                            dve.tensor_reduce(MX[:, c, q, 2 * pair:2 * pair + 2],
                                              PS[:, S_BANKS + 2 * pair:S_BANKS + 2 * pair + 2, 0:w], AX.X, ALU.max)\
                               .then_inc(s_read, 1)
                        if t == FIRST[b + 1] - 1:
                            dve.wait_ge(s_read, g * (2 * STEPS) + 2 * (t + 1))
                            if not (isinstance(g, int) and b == 0):
                                dve.wait_ge(mp_ready, g * NB + b)
                            dve.tensor_reduce(NM[:, :], MX[:, 0:b + 1, :, :].rearrange("p c q j -> p (q j) c"),
                                              AX.X, ALU.max, negate=True).then_inc(nm_ready, 1)

                    def keep_max(g, b):
                        dve.wait_ge(m_turned, g * NB + (b + 1))
                        if not (isinstance(g, int) and b == 0):
                            pb = (b - 1) % NB
                            before = (g * 64 + 64) if b >= 1 else g * 64
                            dve.wait_ge(m_written[pb], before)
                        dve.tensor_copy(MT[:, :], bank_bf(X_BANK)[0:3 * HG, 0:BLK]).then_inc(m_kept, 1)

                    def normalise(g, b):
                        dve.wait_ge(o_turned, g * NB + (b + 1) + 1)
                        o = bank(X_BANK).rearrange("p (q j c) -> p q j c", q=TPB, j=HG)
                        dve.reciprocal(RD[:, :, :], o[:, :, :, DH]).then_inc(recip, 1)
                        dve.wait_ge(recip, g * NB + (b + 1))
                        dst = ATT[:, TPB * b:TPB * (b + 1), bass.ds(g * (HG * DH), HG * DH)]
                        dve.tensor_tensor(dst.rearrange("p q (j d) -> p q j d", d=DH), o[:, :, :, 0:DH],
                                          RD[:, :, :].unsqueeze(3).broadcast_to([P, TPB, HG, DH]), ALU.mult)\
                           .then_inc(normalised, 1)

                    for t in range(LEAD):
                        reduce(0, t)
                        if (t + STEPS - LEAD - 1) % STEPS in M_AT and t >= 1:
                            keep_max(0, M_AT[(t + STEPS - LEAD - 1) % STEPS])
                    for s in from_one["vector"]:
                        dve.sem_inc(s, 1)
                    with dve.Fori(0, NG) as g:
                        for s in range(STEPS):
                            reduce(*lead_of(g, s))
                            if s - 1 in M_AT:
                                b = M_AT[s - 1]
                                keep_max(g if b >= 2 else g + 1, b)
                            if s in O_AT:
                                normalise(g, O_AT[s])
                        normalise(g, NB - 1)

                def keep_output(act, g, b):
                    act.wait_ge(pv_done, g * STEPS + FIRST[b + 1] + 1)
                    act.wait_ge(o_turned, g * NB + b + 1)
                    act.activation(OT[:, :], bank(O_BANK), ACT.Copy).then_inc(o_kept, 1)

                @block.scalar
                def _(act):
                    for s in from_one["scalar"]:
                        act.sem_inc(s, 1)
                    with act.Fori(0, NG) as g:
                        for s in range(STEPS):
                            b, kt, q0 = exp_step(s)
                            for j in range(HG):
                                e = 4 * s + j
                                if j == 0:
                                    act.wait_ge(pv_done, g * STEPS + max(0, s - NSLOT // HG + 1) + 1)
                                act.wait_ge(e_full, g * (4 * STEPS) + (e + 1))
                                act.activation(PR[:, e % NSLOT, 0:BLK - q0], PS[:, E_BANKS + e % 2, 0:BLK - q0],
                                               ACT.Exp, scale=SCALE).then_inc(e_done, 1)
                                if j == 1 and kt == 0 and b >= 1:
                                    keep_output(act, g, b - 1)
                        keep_output(act, g, NB - 1)

                @block.gpsimd
                def _(pool):
                    def load_v(g, b):
                        tiles = slice(TPB * b, TPB * (b + 1))
                        pool.tensor_copy(VG[:, tiles, :, 0:DH + 1], VX[:, tiles, bass.ds(g * HG, HG), :]).then_inc(v_loaded, 1)

                    def split_max(g, b):
                        n = 4 * NB * g + 4 * b
                        wait(pool, nm_ready, g * NB + (b + 1))
                        if not (isinstance(g, int) and b == 0):
                            wait(pool, m_turned, g * NB + b)
                        mp = MP[:, :, :, :].rearrange("p q j n -> p (q j) n")
                        pool.tensor_copy(mp[:, :, 0], NM[:, :]).then_inc(nm_chain, 1)
                        wait(pool, nm_chain, g * (4 * NB) + (4 * b + 1))
                        pool.tensor_tensor(NR[:, 0, :], NM[:, :], mp[:, :, 0], ALU.subtract).then_inc(nm_chain, 1)
                        wait(pool, nm_chain, g * (4 * NB) + (4 * b + 2))
                        pool.tensor_copy(mp[:, :, 1], NR[:, 0, :]).then_inc(nm_chain, 1)
                        wait(pool, nm_chain, g * (4 * NB) + (4 * b + 3))
                        pool.tensor_tensor(NR[:, 1, :], NR[:, 0, :], mp[:, :, 1], ALU.subtract).then_inc(nm_chain, 1)
                        wait(pool, nm_chain, g * (4 * NB) + (4 * b + 4))
                        pool.tensor_copy(mp[:, :, 2], NR[:, 1, :]).then_inc(mp_ready, 1)

                    for b in range(NB):
                        load_v(0, b)
                    split_max(0, 0)
                    split_max(0, 1)
                    with pool.Fori(0, NG) as g:
                        nxt = (g + 1) & (NG - 1)
                        for s in range(STEPS):
                            b, kt, q0 = exp_step(s)
                            n = s - FIRST[NB - 1]
                            if n > 0 and n % TPB == 0:
                                wait(pool, pv_done, g * STEPS + s + 1)
                                load_v(nxt, n // TPB - 1)
                            if kt >= TPB * b:
                                wait(pool, e_done, g * (4 * STEPS) + 4 * (s + 1) + 1)
                                v = PR[:, 4 * s % NSLOT:4 * s % NSLOT + HG, 0:P]
                                pool.affine_select(out=v, in_=v, compare_op=ALU.is_ge, fill=0.0, base=0,
                                                   pattern=[[0, HG], [1, P]], channel_multiplier=-1).then_inc(masked, 1)
                            if s in M_AT:
                                b = M_AT[s]
                                split_max(g if b >= 2 else g + 1, b)
                        wait(pool, pv_done, g * STEPS + STEPS + 1)
                        load_v(nxt, NB - 1)

        def feed_forward(layer):
            L = f"l{layer}_"
            a_turned, a_kept, projected, added = (sem(L + n) for n in ("att_turned", "att_kept", "projected", "added"))
            normed, turned, kept = sem(L + "ff_normed"), sem(L + "ff_turned"), sem(L + "ff_kept")
            hid_full, hid_done, gate_done = sem(L + "hid_full"), sem(L + "hid_done"), sem(L + "gate_done")
            down, chain, stored = sem(L + "down"), sem(L + "ff_chain"), sem(L + "stored")
            var_ready, root_ready = sem(L + "ff_var"), sem(L + "ff_root")
            nh = (C0, C1)[layer]
            AT = work(2048, T)
            HT = [work(4096 + 512 * n, 512) for n in range(2 * nh)]
            GT = [work(8192 + 512 * n, 512) for n in range(2)]

            with nc.Block() as block:
                def wo(pe, b):
                    pe.wait_ge(a_kept, b + 1)
                    if b >= 2:
                        pe.wait_ge(added, b - 1)
                    for t in range(TPB):
                        at = P * (TPB * b + t)
                        last = pe.matmul(PS[:, E_BANKS + b % 2, t * P:(t + 1) * P], AT[:, at:at + P], WO[:, layer, :],
                                         start=True, stop=True)
                    last.then_inc(projected, 1)

                def up(pe, b):
                    pe.wait_ge(kept, b + 1)
                    xs = XNT[:, BLK * b:BLK * (b + 1)]
                    for c in range(nh):
                        for k, w in enumerate((W1T,) if layer == 0 else (WGT, WUT)):
                            n = ((1, 2)[layer]) * (nh * b + c) + k
                            if n >= 4:
                                pe.wait_ge(hid_done if layer == 0 or k else gate_done,
                                           n - 3 if layer == 0 else (n - 4) // 2 + 1)
                            pe.matmul(bank(n % 4), w[:, c * P:(c + 1) * P], xs, start=True, stop=True).then_inc(hid_full, 1)

                def back(pe, b):
                    pe.wait_ge(hid_done, nh * (b + 1))
                    pe.wait_ge(added, NB)
                    if b >= 2:
                        pe.wait_ge(added, NB + b - 1)
                    w = (W2T, WDT)[layer]
                    for t in range(TPB):
                        for c in range(nh):
                            last = pe.matmul(PS[:, E_BANKS + b % 2, t * P:(t + 1) * P],
                                             HT[nh * (b % 2) + c][:, t * P:(t + 1) * P], w[:, c, :],
                                             start=(c == 0), stop=(c == nh - 1))
                    last.then_inc(down, 1)

                @block.tensor
                def _(pe):
                    for b in range(NB):
                        if b >= 2:
                            pe.wait_ge(a_kept, b - 1)
                        for t in range(TPB):
                            last = pe.transpose(PS[:, O_BANK + b % 2, t * P:(t + 1) * P], ATT[:, TPB * b + t, :], IDF[:, :])
                        last.then_inc(a_turned, 1)
                        if b >= 1:
                            wo(pe, b - 1)
                    wo(pe, NB - 1)
                    for b in range(NB):
                        pe.wait_ge(normed, b + 1)
                        pe.wait_ge(a_kept, NB)
                        if b >= 2:
                            pe.wait_ge(kept, b - 1)
                        for t in range(TPB):
                            last = pe.transpose(PS[:, O_BANK + b % 2, t * P:(t + 1) * P], XN[:, TPB * b + t, :], IDF[:, :])
                        last.then_inc(turned, 1)
                        up(pe, b)
                        if b >= 1:
                            back(pe, b - 1)
                    back(pe, NB - 1)

                @block.scalar
                def _(act):
                    for b in range(NB):
                        act.wait_ge(a_turned, b + 1)
                        act.activation(AT[:, BLK * b:BLK * (b + 1)], bank(O_BANK + b % 2), ACT.Copy).then_inc(a_kept, 1)
                    for b in range(NB):
                        root(act, b, var_ready, root_ready)
                    for b in range(NB):
                        act.wait_ge(turned, b + 1)
                        act.activation(XNT[:, BLK * b:BLK * (b + 1)], bank(O_BANK + b % 2), ACT.Copy).then_inc(kept, 1)
                        for c in range(nh):
                            n = nh * b + c
                            if layer == 0:
                                act.wait_ge(hid_full, n + 1)
                                if b >= 2:
                                    act.wait_ge(down, b - 1)
                                act.activation(HT[nh * (b % 2) + c], bank(n % 4), ACT.Gelu, bias=B1[:, c:c + 1])\
                                   .then_inc(hid_done, 1)
                            else:
                                act.wait_ge(hid_full, 2 * n + 1)
                                if n >= 2:
                                    act.wait_ge(hid_done, n - 1)
                                act.activation(GT[n % 2], bank(2 * n % 4), ACT.Silu).then_inc(gate_done, 1)

                def add(dve, link, b):
                    dve.wait_ge(down, b + 1)
                    x = X[:, TPB * b:TPB * (b + 1), :]
                    o = bank(E_BANKS + b % 2).rearrange("p (t d) -> p t d", t=TPB)
                    if layer == 0:
                        tmp = XN[:, TPB * b:TPB * (b + 1), :]
                        link(dve.tensor_tensor(tmp, o, B2[:, :].unsqueeze(1).broadcast_to([P, TPB, D]), ALU.add))
                        dve.tensor_tensor(x, x, tmp, ALU.add).then_inc(added, 1)
                    else:
                        dve.tensor_tensor(x, x, o, ALU.add).then_inc(added, 1)

                @block.vector
                def _(dve):
                    link = Chain(dve, chain)
                    for b in range(NB):
                        dve.wait_ge(projected, b + 1)
                        x = X[:, TPB * b:TPB * (b + 1), :].rearrange("p t d -> p (t d)")
                        dve.tensor_tensor(x, x, bank(E_BANKS + b % 2), ALU.add).then_inc(added, 1)
                        dve.wait_ge(added, b + 1)
                        dve.wait_ge(a_turned, b + 1)
                        row_statistics(dve, link, b, var_ready)
                        if b >= 1:
                            normalise_rows(dve, link, b - 1, root_ready).then_inc(normed, 1)
                    normalise_rows(dve, link, NB - 1, root_ready).then_inc(normed, 1)
                    for b in range(NB):
                        if layer == 1:
                            for c in range(nh):
                                n = nh * b + c
                                dve.wait_ge(gate_done, n + 1)
                                dve.wait_ge(hid_full, 2 * n + 2)
                                if b >= 2:
                                    dve.wait_ge(down, b - 1)
                                dve.tensor_tensor(HT[nh * (b % 2) + c], GT[n % 2], bank((2 * n + 1) % 4), ALU.mult)\
                                   .then_inc(hid_done, 1)
                            if b >= 1:
                                add(dve, link, b - 1)
                        else:
                            add(dve, link, b)
                    if layer == 1:
                        add(dve, link, NB - 1)

                @block.sync
                def _(sp):
                    if layer == 1:
                        for b in range(NB):
                            sp.wait_ge(added, NB + b + 1)
                            sp.dma_start(out[0, BLK * b:BLK * (b + 1), :].rearrange("(i p) d -> p i d", p=P),
                                         X[:, TPB * b:TPB * (b + 1), :]).then_inc(stored, 16)
                        sp.wait_ge(stored, 16 * NB)

        for layer in range(2):
            attention_operands(layer)
            attention(layer)
            feed_forward(layer)


_INS = ['L0_attn_x', 'L0_attn_w_qkv', 'L0_attn_w_o', 'L0_attn_log_scale', 'L0_ffn_w1', 'L0_ffn_b1', 'L0_ffn_w2',
        'L0_ffn_b2', 'L1_attn_W_q', 'L1_attn_W_k', 'L1_attn_W_v', 'L1_attn_W_o', 'L1_ffn_w_gate', 'L1_ffn_w_up',
        'L1_ffn_w_down']


def kernel(**inputs):
    import numpy as _np
    import concourse.bacc as _bacc
    from concourse import mybir as _mybir
    from concourse.bass_utils import run_bass_kernel_spmd as _run

    nc = _bacc.Bacc("TRN2", target_bir_lowering=False, num_devices=1)
    arrays, args = {}, []
    for name in _INS:
        a = _np.ascontiguousarray(inputs[name])
        arrays[f"in_{name}"] = a
        args.append(nc.dram_tensor(f"in_{name}", a.shape, _mybir.dt.from_np(a.dtype), kind="ExternalInput").ap())
    args.append(nc.dram_tensor("out_x", (1, T, D), _mybir.dt.float32, kind="ExternalOutput").ap())
    build(nc, *args)
    r = _run(nc, [arrays], core_ids=[0])
    return r.results[0]["out_x"]
```

```python
from contextlib import ExitStack

import numpy as np

import concourse.bass as bass
from concourse import mybir

FP32, BF16, I32 = mybir.dt.float32, mybir.dt.bfloat16, mybir.dt.int32
ALU = mybir.AluOpType
ACT = mybir.ActivationFunctionType
AX = mybir.AxisListType

P = 128
T, D = 2048, 128
H, DH = 16, 8
NT = T // P
BLK = 512
TPB = BLK // P
NB = T // BLK
TPU = 2
NU = NT // TPU
HG = 4
NG = H // HG
ROWS = 64
MROW = 48
VW = 32
HID0, HID1 = 512, 384
C0, C1 = HID0 // P, HID1 // P
EPS = 1e-5
SCALE = float(DH) ** -0.5
NEG = -1e30

FIRST = [sum(TPB * (q + 1) for q in range(b)) for b in range(NB + 1)]
STEPS = FIRST[NB]
LEAD = 20
LAG = 2
NSLOT = 16
S_BANKS, E_BANKS, O_BANK, X_BANK = 0, 4, 6, 7
TURNING = (4, 5, 7)


def block_of(step):
    return max(b for b in range(NB) if FIRST[b] <= step)


def rope_frequencies():
    gamma = np.asarray((14.134725142, 21.022039639, 25.01085758, 30.424876126), np.float32)
    inv0 = np.float32(1.0) / (gamma / gamma[0])
    inv1 = np.float32(10000.0) ** (np.float32(-2.0) * np.arange(DH // 2, dtype=np.float32) / np.float32(DH))
    return [float(v) for v in inv0], [float(v) for v in inv1.astype(np.float32)]


def wait(eng, sem, value):
    eng.wait_ge(sem, value)
    eng.sem_inc(wait.passed, 1)


class Chain:

    def __init__(self, eng, sem):
        self.eng, self.sem, self.n = eng, sem, 0

    def __call__(self, ins):
        self.n += 1
        ins.then_inc(self.sem, 1)
        self.eng.wait_ge(self.sem, self.n)

    def mark(self, ins):
        self.n += 1
        ins.then_inc(self.sem, 1)
        return self.n


def build(nc, x_in, w_qkv, w_o0, log_scale, w1, b1, w2, b2, w_q, w_k, w_v, w_o1, w_gate, w_up, w_down, out):
    ctx = ExitStack()
    with ctx:
        def sb(name, shape, dt):
            return ctx.enter_context(nc.sbuf_tensor(name, shape, dt))

        def sem(name):
            return ctx.enter_context(nc.semaphore(name))

        X = sb("x_res", [P, NT, D], FP32)
        XN = sb("x_norm", [P, NT, D], FP32)
        ATT = XN
        VX = sb("v_all", [P, NT, H, DH + 1], FP32)
        QA = sb("q_all", [P, H // 2, T], BF16)
        KA = sb("k_all", [P, H // 2, T], BF16)
        Q2 = sb("q_group", [P, HG // 2, T], BF16)
        K2 = sb("k_group", [P, HG, T], BF16)
        Q1 = sb("q_group_max", [P, T], BF16)
        K1 = sb("k_group_max", [P, T], BF16)
        VG = sb("v_group", [P, NT, HG, VW], FP32)
        WORK = sb("work", [P, 11264], FP32)
        SIN = sb("sin", [P, 2, NT, H * DH // 2], FP32)
        COS = sb("cos", [P, 2, NT, H * DH // 2], FP32)
        WQKV = sb("w_qkv_sb", [P, 2, 3 * D], FP32)
        WO = sb("w_o_sb", [P, 2, D], FP32)
        W1T = sb("w1_t", [P, HID0], FP32)
        W2T = sb("w2_t", [P, C0, D], FP32)
        WGT = sb("w_gate_t", [P, HID1], FP32)
        WUT = sb("w_up_t", [P, HID1], FP32)
        WDT = sb("w_down_t", [P, C1, D], FP32)
        B1 = sb("b1_sb", [P, C0], FP32)
        B2 = sb("b2_sb", [P, D], FP32)
        IDF = sb("ident_f", [P, P], FP32)
        IDB = sb("ident_b", [P, P], BF16)
        CM = sb("causal_b", [P, P], BF16)
        STAT = sb("ln_stat", [P, NT, 6], FP32)
        MV = sb("ln_mv", [P, NT, 2], FP32)
        VAR = sb("ln_var", [P, NT], FP32)
        ROOT = sb("ln_root", [P, NT], FP32)
        RSTD = sb("ln_rstd", [P, NT], FP32)
        MX = sb("max_parts", [P, NB, TPB, HG], FP32)
        NM = sb("neg_max", [P, TPB * HG], FP32)
        NR = sb("neg_max_rest", [P, 2, TPB * HG], FP32)
        MP = sb("neg_max_bf", [P, TPB, HG, 3], BF16)
        MT = sb("neg_max_rows", [HG * 3, 2, BLK], BF16)
        RD = sb("o_recip", [P, TPB, HG], FP32)

        PS = ctx.enter_context(nc.psum_tensor("ps", [P, 8, 512], FP32))

        def bank(n):
            return PS[:, n, :]

        def bank_bf(n):
            return PS[:, n, :].bitcast(BF16)

        def work(at, n):
            return WORK[:, at:at + n]

        PR = WORK[:, 0:NSLOT * BLK].rearrange("p (s n) -> p s n", s=NSLOT)

        OT = work(NSLOT * BLK, BLK)
        XNT = work(9216, T)

        inv0, inv1 = rope_frequencies()

        ld_x = [sem(f"x_loaded{b}") for b in range(NB)]
        ld_w, ld_b = sem("weights_loaded"), sem("biases_loaded")
        ident_ready, pos_ready, scale_ready = sem("ident_ready"), sem("pos_ready"), sem("scale_ready")
        wait.passed = sem("waits_passed")
        pool_chain, dve_chain = sem("setup_pool_chain"), sem("setup_dve_chain")
        theta_ready, sin_ready, sq_ready = sem("theta_ready"), sem("sin_ready"), sem("sq_ready")
        raw_ready, w_turned, w_kept = sem("raw_ready"), sem("w_turned"), sem("w_kept")

        S1 = work(0, 512).rearrange("p (c n) -> p c n", c=C0)
        S2 = work(512, 512)
        SA = work(1024, 512).rearrange("p (c n) -> p c n", c=4)
        SI = [work(1536 + 384 * i, 384).bitcast(I32).rearrange("p (c n) -> p c n", c=C1) for i in range(3)]
        SF = [work(2688 + 384 * i, 384).rearrange("p (c n) -> p c n", c=C1) for i in range(3)]
        SG1, SG2 = work(3840, 512), work(4352, 512)
        TH = work(4864, 2048)
        KK = work(6912, 2048)
        POSI = work(8960, 16).bitcast(I32)
        POSF = work(8976, 16)
        TH0 = work(8992, 64).rearrange("p (i f) -> p i f", f=4)
        LSC = work(9056, 16)
        ESC = work(9072, 16)
        AL = work(9088, 8)

        with nc.Block() as block:
            @block.sync
            def _(sp):
                for b in range(NB):
                    sp.dma_start(X[:, TPB * b:TPB * (b + 1), :],
                                 x_in[0, BLK * b:BLK * (b + 1), :].rearrange("(i p) d -> p i d", p=P)).then_inc(ld_x[b], 16)
                sp.dma_start(S1, w1.rearrange("(c p) d -> p c d", p=P)).then_inc(ld_w, 16)
                sp.dma_start(S2, w2).then_inc(ld_w, 16)
                for n, w in enumerate((w_gate, w_up)):
                    sp.dma_start(SI[n], w.rearrange("(c p) d -> p c d", p=P)).then_inc(ld_w, 16)
                sp.dma_start(SI[2], w_down.rearrange("p (c n) -> p c n", c=C1)).then_inc(ld_w, 16)
                for n, w in enumerate((w_q, w_k, w_v, w_o1)):
                    sp.dma_start(SA[:, n, :], w).then_inc(ld_w, 16)
                sp.dma_start(WQKV[:, 0, :], w_qkv).then_inc(ld_w, 16)
                sp.dma_start(WO[:, 0, :], w_o0).then_inc(ld_w, 16)
                for b in range(NB):
                    sp.wait_ge(ld_x[b], 16)

            @block.gpsimd
            def _(pool):
                link = Chain(pool, pool_chain)
                pool.iota(POSI, pattern=[[P, NT]], base=0, channel_multiplier=1).then_inc(pos_ready, 1)
                pool.memset(IDF[:, :], 0.0).then_inc(pool_chain, 1)
                pool.memset(IDB[:, :], 0.0).then_inc(pool_chain, 1)
                pool.memset(CM[:, :], 0.0).then_inc(pool_chain, 1)
                pool.memset(VG[:, :, :, :], 0.0)
                pool.memset(K2[:, :, :], 0.0)
                pool.memset(VX[:, :, :, DH:DH + 1], 1.0)
                pool.wait_ge(pool_chain, 3)
                for m in (IDF, IDB):
                    pool.affine_select(out=m[:, :], in_=m[:, :], compare_op=ALU.not_equal, fill=1.0,
                                       base=0, pattern=[[-1, P]], channel_multiplier=1).then_inc(ident_ready, 1)
                pool.affine_select(out=CM[:, :], in_=CM[:, :], compare_op=ALU.is_ge, fill=NEG,
                                   base=0, pattern=[[-1, P]], channel_multiplier=1).then_inc(ident_ready, 1)

            @block.scalar
            def _(act):
                act.dma_start(LSC, log_scale.rearrange("(a n) -> a n", a=1).broadcast_to([P, H])).then_inc(ld_b, 16)
                act.dma_start(B1[:, :], b1.rearrange("(c p) -> p c", p=P), allow_slow_non_contiguous=True).then_inc(ld_b, 16)
                act.dma_start(B2[:, :], b2.rearrange("(a n) -> a n", a=1).broadcast_to([P, D])).then_inc(ld_b, 16)
                act.wait_ge(ld_b, 48)
                act.activation(ESC, LSC, ACT.Exp).then_inc(scale_ready, 1)
                act.wait_ge(theta_ready, 1)
                act.activation(SIN[:, :, :, :].rearrange("p l i m -> p (l i m)"), TH, ACT.Sin).then_inc(sin_ready, 1)
                act.activation(KK, TH, ACT.Sin, scale=0.5).then_inc(sin_ready, 1)
                for n, dst in enumerate((W1T[:, :], W2T[:, :, :].rearrange("p c n -> p (c n)"),
                                         None, WGT[:, :], WUT[:, :], WDT[:, :, :].rearrange("p c n -> p (c n)"))):
                    act.wait_ge(w_turned, n + 1)
                    if dst is None:
                        act.activation(WQKV[:, 1, :], PS[:, n, 0:3 * D], ACT.Copy).then_inc(w_kept, 1)
                        act.activation(WO[:, 1, :], PS[:, n, 3 * D:4 * D], ACT.Copy).then_inc(w_kept, 1)
                    else:
                        act.activation(dst, PS[:, n, 0:dst.shape[1]], ACT.Copy).then_inc(w_kept, 1)
                act.wait_ge(w_kept, 7)

            @block.vector
            def _(dve):
                link = Chain(dve, dve_chain)
                dve.wait_ge(pos_ready, 1)
                link(dve.tensor_copy(POSF, POSI))
                for layer, inv in enumerate((inv0, inv1)):
                    for f in range(DH // 2):
                        link(dve.tensor_scalar(TH0[:, :, f], POSF, inv[f], None, ALU.mult))
                    th = TH.rearrange("p (l i h f) -> p l i h f", l=2, i=NT, h=H)[:, layer]
                    t0 = TH0.unsqueeze(2).broadcast_to([P, NT, H, DH // 2])
                    if layer == 0:
                        dve.wait_ge(scale_ready, 1)
                        e = ESC.unsqueeze(1).unsqueeze(3).broadcast_to([P, NT, H, DH // 2])
                        link(dve.tensor_tensor(th, t0, e, ALU.mult))
                    else:
                        link(dve.tensor_copy(th, t0))
                magic = 1.5 * 2.0 ** 23
                parts = (6.28125, float(np.float32(2 * np.pi - 6.28125).astype(np.float32)), 0.0)
                c2 = float(np.float32(np.round((2 * np.pi - 6.28125) * 2 ** 21) / 2 ** 21))
                c3 = float(np.float32(2 * np.pi - 6.28125 - c2))
                link(dve.tensor_scalar(KK, TH, float(1 / (2 * np.pi)), magic, ALU.mult, ALU.add))
                link(dve.tensor_scalar(KK, KK, magic, None, ALU.subtract))
                for c in (parts[0], c2, c3):
                    link(dve.scalar_tensor_tensor(out=TH, in0=KK, scalar=-c, in1=TH, op0=ALU.mult, op1=ALU.add))
                dve.tensor_scalar(TH, TH, 3.1415925, -3.1415925, ALU.min, ALU.max).then_inc(theta_ready, 1)
                dve.wait_ge(ld_w, 16 * 11)
                for n, (s, red) in enumerate(((S1, P), (S2.unsqueeze(1), HID0))):
                    c = s.shape[1]
                    al = AL[:, 4 * n:4 * n + c]
                    g1 = SG1.rearrange("p (c n) -> p c n", c=c)
                    g2 = SG2.rearrange("p (c n) -> p c n", c=c)
                    link(dve.tensor_reduce(al, s, AX.X, ALU.add, apply_absolute_value=True))
                    link(dve.tensor_scalar(al, al, 1.0 / red, None, ALU.mult))
                    link(dve.tensor_scalar(g1, s, 0.0, None, ALU.is_gt))
                    link(dve.tensor_scalar(g2, s, 0.0, None, ALU.is_lt))
                    link(dve.tensor_tensor(g1, g1, g2, ALU.subtract))
                    link(dve.tensor_tensor(g1, g1, al.unsqueeze(2).broadcast_to([P, c, 512 // c]), ALU.mult))
                    link(dve.tensor_tensor(g1, g1, s, ALU.subtract))
                    link(dve.tensor_tensor(s, s, g1, ALU.add))
                for n in range(3):
                    link(dve.tensor_scalar(SF[n], SI[n], float(np.float32(1.0 / 127.0)), None, ALU.mult))
                dve.sem_inc(raw_ready, 1)
                dve.wait_ge(sin_ready, 2)
                link(dve.tensor_tensor(KK, KK, KK, ALU.mult))
                link(dve.tensor_scalar(COS[:, :, :, :].rearrange("p l i m -> p (l i m)"), KK, -2.0, 1.0,
                                       ALU.mult, ALU.add))

            @block.tensor
            def _(pe):
                pe.wait_ge(ident_ready, 3)
                pe.wait_ge(raw_ready, 1)
                groups = [[S1[:, c, :] for c in range(C0)], [S2[:, c * P:(c + 1) * P] for c in range(C0)],
                          [SA[:, n, :] for n in range(4)]] + [[SF[n][:, c, :] for c in range(C1)] for n in range(3)]
                for n, group in enumerate(groups):
                    for c, src in enumerate(group):
                        last = pe.transpose(PS[:, n, c * P:(c + 1) * P], src, IDF[:, :])
                    last.then_inc(w_turned, 1)

        def row_statistics(dve, link, b, var_ready):
            ts = slice(TPB * b, TPB * (b + 1))
            for i in range(TPB * b, TPB * (b + 1)):
                n = link.mark(dve.bn_stats(STAT[:, i, :], X[:, i, :]))
            for i in range(TPB * b, TPB * (b + 1)):
                dve.wait_ge(link.sem, n)
                m = link.mark(dve.bn_aggr(MV[:, i, :], STAT[:, i, :]))
            dve.wait_ge(link.sem, m)
            dve.tensor_scalar(VAR[:, ts], MV[:, ts, 1], EPS, None, ALU.add).then_inc(var_ready, 1)

        def root(act, b, var_ready, root_ready):
            ts = slice(TPB * b, TPB * (b + 1))
            act.wait_ge(var_ready, b + 1)
            act.activation(ROOT[:, ts], VAR[:, ts], ACT.Sqrt).then_inc(root_ready, 1)

        def normalise_rows(dve, link, b, root_ready):
            ts = slice(TPB * b, TPB * (b + 1))
            dve.wait_ge(root_ready, b + 1)
            link(dve.reciprocal(RSTD[:, ts], ROOT[:, ts]))
            link(dve.tensor_tensor(ROOT[:, ts], RSTD[:, ts], RSTD[:, ts], ALU.mult))
            link(dve.tensor_tensor(ROOT[:, ts], ROOT[:, ts], VAR[:, ts], ALU.mult))
            link(dve.tensor_scalar(ROOT[:, ts], ROOT[:, ts], -0.5, 1.5, ALU.mult, ALU.add))
            link(dve.tensor_tensor(RSTD[:, ts], RSTD[:, ts], ROOT[:, ts], ALU.mult))
            for i in range(TPB * b, TPB * (b + 1)):
                last = dve.tensor_scalar(XN[:, i, :], X[:, i, :], MV[:, i, 0:1], RSTD[:, i:i + 1],
                                         ALU.subtract, ALU.mult)
            return last

        def attention(layer):
            L = f"l{layer}_"
            p1_loaded = [sem(f"{L}max_operands{b}") for b in range(NB)]
            p2_loaded = [sem(f"{L}operands{b}") for b in range(NB)]
            m_written = [sem(f"{L}max_rows{b}") for b in range(NB)]
            v_loaded = sem(L + "v_group")
            s_full, s_read = sem(L + "scores_full"), sem(L + "scores_read")
            nm_ready, nm_chain, mp_ready = sem(L + "neg_max"), sem(L + "split_chain"), sem(L + "max_split")
            m_turned, m_kept = sem(L + "max_turned"), sem(L + "max_kept")
            e_full, e_done, masked = sem(L + "exp_in"), sem(L + "exp_done"), sem(L + "masked")
            pv_done, o_kept, o_turned = sem(L + "pv_done"), sem(L + "o_kept"), sem(L + "o_turned")
            recip, normalised = sem(L + "recip"), sem(L + "normalised")
            normed, turned, kept = sem(L + "normed"), sem(L + "xn_turned"), sem(L + "xn_kept")
            var_ready, root_ready = sem(L + "var"), sem(L + "root")
            qkv_ready, qk_kept, v_kept = sem(L + "qkv_ready"), sem(L + "qk_kept"), sem(L + "v_kept")
            chain, rotated, rest1, rest2 = sem(L + "op_chain"), sem(L + "rotated"), sem(L + "rest1"), sem(L + "rest2")
            high, mid, low, doubled = sem(L + "high"), sem(L + "mid"), sem(L + "low"), sem(L + "doubled")
            edge, stacked, stored = sem(L + "edge"), sem(L + "stacked"), sem(L + "stacks_stored")

            QK = work(0, NU * 512).rearrange("p (u t a n) -> p u t a n", u=NU, t=TPU, a=2)
            ROT = [work(4096 + 512 * n, 512).rearrange("p (t a n) -> p t a n", t=TPU, a=2) for n in range(2)]
            tmp = [work(5120 + 256 * n, 256).rearrange("p (t a m) -> p t a m", t=TPU, a=2) for n in range(4)]
            R1, R2 = work(6144, 512), work(6656, 512)
            ASM = [work(7168 + 2048 * n, 2048).bitcast(BF16).rearrange("p (t a h c) -> p t a h c", t=TPU, a=2, h=H)
                   for n in range(2)]

            def rows_of(v):
                return v.rearrange("p (r d) -> p r d", d=DH)

            def rot_rows(u):
                return rows_of(ROT[u % 2].rearrange("p t a n -> p (t a n)"))

            def asm_rows(u, n):
                return ASM[u % 2].rearrange("p t a h c -> p (t a h) c")[:, :, DH * n:DH * (n + 1)]

            def part(u, a, n):
                return ASM[u % 2][:, :, a, :, DH * n:DH * (n + 1)]

            BESIDE = {3: range(0, 2), 4: range(2, 4), 5: range(4, 6), 6: range(6, 9), 7: range(9, 12)}
            BEHIND = range(12, LEAD)

            M_END = {FIRST[b + 1] - 1: b for b in range(NB)}
            M_TURN, O_TURN, O_KEEP = 2, 4, 2

            def max_step(t):
                b = block_of(t)
                c, q = divmod(t - FIRST[b], TPB)
                return b, c, q, (BLK if c < b else P * (q + 1))

            def exp_step(s):
                b = block_of(s)
                kt = s - FIRST[b]
                return b, kt, P * max(0, kt - TPB * b)

            def beside(g, s, nxt):
                return (g, s + LEAD) if s < LEAD else (nxt, s - LEAD) if nxt is not None else None

            def maxima_ended(g, s, nxt, ago):
                t = s + LEAD - ago
                who, t = (g, t) if t < STEPS else (nxt, t - STEPS)
                return (who, M_END[t]) if t in M_END and who is not None else None

            def block_ended(g, s, prev, ago):
                t = s - ago
                who, t = (g, t) if t >= 0 else (prev, t + STEPS)
                return (who, M_END[t]) if t in M_END and who is not None else None

            def drive(eng, step):
                for s in range(LEAD):
                    step(0, s, None, None)
                with eng.Fori(0, NG - 1) as g:
                    for s in range(LEAD, STEPS):
                        step(g, s, None, g + 1)
                    for s in range(LEAD):
                        step(g + 1, s, g, None)
                for s in range(LEAD, STEPS):
                    step(NG - 1, s, None, None)

            def wait_for(eng, sem, value):
                if not (isinstance(value, int) and value <= 0):
                    if eng.engine in (mybir.EngineType.Pool, mybir.EngineType.SP):
                        wait(eng, sem, value)
                    else:
                        eng.wait_ge(sem, value)

            USES = []
            for s in range(STEPS):
                USES += [(s, "exp", j) for j in range(HG)]
                USES += [(s, "max", M_END[e]) for e in M_END if (e - LEAD + M_TURN - s) % STEPS == 0]
                USES += [(s, "out", M_END[e]) for e in M_END if (e + O_TURN - s) % STEPS == 0]
            assert len(USES) % len(TURNING) == 0

            def turning_bank(s, kind, n):
                return TURNING[USES.index((s % STEPS, kind, n)) % len(TURNING)]

            def max_bank(g, b):
                at = FIRST[b + 1] - 1 - LEAD + M_TURN
                return X_BANK if isinstance(g, int) and g == 0 and at < 0 else turning_bank(at, "max", b)

            def out_bank(b):
                return turning_bank(FIRST[b + 1] - 1 + O_TURN, "out", b)

            def bank_free(g, s, kind, n, prev):
                at = USES.index((s, kind, n)) - len(TURNING)
                while True:
                    if at < 0 and prev is None:
                        return e_done, 0
                    s, kind, n = USES[at % len(USES)]
                    before = 0 if at >= 0 else -1
                    if kind == "exp":
                        return e_done, g * (4 * STEPS) + (before * 4 * STEPS + 4 * s + n + 1)
                    if kind == "max":
                        ahead = 1 if s >= LEAD + M_TURN else 0
                        if not (isinstance(g, int) and g + before + ahead == NG):
                            return m_kept, g * NB + ((before + ahead) * NB + n + 1)
                    if kind == "out":
                        behind = 1 if s < O_TURN else 0
                        if not (isinstance(g, int) and g + before - behind < 0):
                            return normalised, g * NB + ((before - behind) * NB + n + 1)
                    at -= len(TURNING)

            with nc.Block() as block:
                @block.sync
                def _(sp):
                    def load_max(g, b):
                        cols = slice(BLK * b, BLK * (b + 1))
                        for j in range(HG):
                            rows = slice(ROWS * (j % 2), ROWS * (j % 2) + 32)
                            for dst, src in ((Q1, QA), (K1, KA)):
                                sp.dma_start(dst[32 * j:32 * j + 32, cols],
                                             src[rows, bass.ds(g * 2 + j // 2, 1), cols].squeeze(1))\
                                  .then_inc(p1_loaded[b], 16)

                    def load_exp(g, b):
                        cols = slice(BLK * b, BLK * (b + 1))
                        for j in range(2):
                            rows = slice(ROWS * j, ROWS * (j + 1))
                            sp.dma_start(K2[rows, j:HG:2, cols], KA[rows, bass.ds(g * 2, 2), cols]).then_inc(p2_loaded[b], 16)
                        sp.dma_start(Q2[:, :, cols], QA[:, bass.ds(g * 2, 2), cols]).then_inc(p2_loaded[b], 16)

                    def write_max(g, b):
                        wait_for(sp, m_kept, g * NB + (b + 1))
                        wait_for(sp, p2_loaded[b], g * 48 + 48)
                        for j in range(HG):
                            at = ROWS * (j % 2) + MROW
                            sp.dma_start(Q2[at:at + 3, j // 2, BLK * b:BLK * (b + 1)], MT[3 * j:3 * j + 3, b % 2, :])\
                              .then_inc(m_written[b], 16)

                    for b in range(NB):
                        sp.wait_ge(stored, 8 * (b + 1))
                        load_max(0, b)
                        load_exp(0, b)
                    write_max(0, 0)
                    write_max(0, 1)
                    with sp.Fori(0, NG - 1) as g:
                        write_max(g, 2)
                        for b in range(NB):
                            wait_for(sp, s_full, g * (2 * STEPS) + 2 * (FIRST[NB - 1] + TPB * (b + 1)))
                            load_max(g + 1, b)
                        write_max(g, 3)
                        for b in range(NB):
                            wait_for(sp, e_full, g * (4 * STEPS) + 4 * (FIRST[NB - 1] + TPB * (b + 1)))
                            load_exp(g + 1, b)
                            if b < 2:
                                write_max(g + 1, b)
                    write_max(NG - 1, 2)
                    write_max(NG - 1, 3)
                    for b in range(NB):
                        sp.wait_ge(p1_loaded[b], 128 * NG)
                        sp.wait_ge(p2_loaded[b], 48 * NG)
                        sp.wait_ge(m_written[b], 64 * NG)

                @block.tensor
                def _(pe):
                    def maxima(g, t, pairs=(0, 1)):
                        b, c, q, w = max_step(t)
                        if t == FIRST[b] and 0 in pairs:
                            wait_for(pe, p1_loaded[b], g * 128 + 128)
                        at = P * (TPB * b + q)
                        for pair in pairs:
                            wait_for(pe, s_read, g * (2 * STEPS) + (2 * t + pair - 1))
                            for j in (2 * pair, 2 * pair + 1):
                                rows = slice(32 * j, 32 * j + 32)
                                last = pe.matmul(PS[:, S_BANKS + j, 0:w], Q1[rows, at:at + P],
                                                 K1[rows, BLK * c:BLK * c + w], start=True, stop=(c < b))
                            if c == b:
                                for j in (2 * pair, 2 * pair + 1):
                                    last = pe.matmul(PS[:, S_BANKS + j, w - P:w], IDB[:, :], CM[:, :],
                                                     start=False, stop=True)
                            last.then_inc(s_full, 1)

                    def turn_max(g, b, at=None):
                        wait_for(pe, mp_ready, g * NB + (b + 1))
                        if at is None:
                            wait_for(pe, m_kept, b)
                        else:
                            wait_for(pe, *bank_free(*at))
                        for q in range(TPB):
                            last = pe.transpose(bank_bf(max_bank(g, b))[0:3 * HG, q * P:(q + 1) * P],
                                                MP[:, q, :, :].rearrange("p j n -> p (j n)"), IDB[:, :])
                        last.then_inc(m_turned, 1)

                    def scores(g, s, j, prev):
                        b, kt, q0 = exp_step(s)
                        if kt == 0 and j == 0:
                            wait_for(pe, p2_loaded[b], g * 48 + 48)
                            wait_for(pe, m_written[b], g * 64 + 64)
                        wait_for(pe, *bank_free(g, s, "exp", j, prev))
                        pe.matmul(PS[:, turning_bank(s, "exp", j), 0:BLK - q0], K2[:, j, kt * P:(kt + 1) * P],
                                  Q2[:, j // 2, BLK * b + q0:BLK * (b + 1)], start=True, stop=True).then_inc(e_full, 1)

                    def product(g, s):
                        b, kt, q0 = exp_step(s)
                        if kt == 0:
                            wait_for(pe, o_kept, g * NB + b)
                            wait_for(pe, v_loaded, g * NB + (b + 1))
                        wait_for(pe, e_done, g * (4 * STEPS) + 4 * (s + 1))
                        if kt >= TPB * b:
                            wait_for(pe, masked, g * NT + (kt + 1))
                        for j in range(HG):
                            last = pe.matmul(PS[VW * j:VW * (j + 1), O_BANK, q0:BLK], VG[:, kt, j, :],
                                             PR[:, (4 * s + j) % NSLOT, 0:BLK - q0],
                                             start=(kt == 0), stop=(kt == TPB * (b + 1) - 1))
                        last.then_inc(pv_done, 1)

                    def turn_output(g, b, at=None):
                        wait_for(pe, o_kept, g * NB + (b + 1))
                        if at is not None:
                            wait_for(pe, *bank_free(*at))
                        for q in range(TPB):
                            last = pe.transpose(PS[:, out_bank(b), q * P:(q + 1) * P], OT[:, q * P:(q + 1) * P], IDF[:, :])
                        last.then_inc(o_turned, 1)

                    def lead(g, t):
                        maxima(g, t)
                        if t - M_TURN in M_END:
                            turn_max(g, M_END[t - M_TURN])

                    def step(g, s, prev, nxt):
                        at = beside(g, s, nxt)
                        scores(g, s, 0, prev)
                        if at:
                            maxima(*at, (0,))
                        scores(g, s, 1, prev)
                        if s >= LAG:
                            product(g, s - LAG)
                        elif prev is not None:
                            product(prev, STEPS + s - LAG)
                        scores(g, s, 2, prev)
                        if at:
                            maxima(*at, (1,))
                        scores(g, s, 3, prev)
                        if who := maxima_ended(g, s, nxt, M_TURN):
                            turn_max(*who, (g, s, "max", who[1], prev))
                        if who := block_ended(g, s, prev, O_TURN):
                            turn_output(*who, (g, s, "out", who[1], prev))

                    def turn(b):
                        pe.wait_ge(normed, b + 1)
                        if b >= 2:
                            pe.wait_ge(kept, b - 1)
                        for t in range(TPB):
                            last = pe.transpose(PS[:, O_BANK + b % 2, t * P:(t + 1) * P], XN[:, TPB * b + t, :], IDF[:, :])
                        last.then_inc(turned, 1)

                    def project(u):
                        pe.wait_ge(kept, u // 2 + 1)
                        if u >= 2:
                            pe.wait_ge(v_kept, u - 1)
                        for t in range(TPU):
                            at = P * (TPU * u + t)
                            last = pe.matmul(PS[:, TPU * (u % 2) + t, 0:3 * D], XNT[:, at:at + P], WQKV[:, layer, :],
                                             start=True, stop=True)
                        last.then_inc(qkv_ready, 1)

                    def stack(u):
                        pe.wait_ge(low, u + 1)
                        pe.wait_ge(doubled, u + 1)
                        pe.wait_ge(edge, 2 + 2 * min(u, 1))
                        for f in range(4):
                            n = 4 * u + f
                            if n >= 3:
                                pe.wait_ge(stored, n - 2)
                            for k in range(4):
                                for t in range(TPU):
                                    h = 8 * (f % 2) + 2 * k
                                    last = pe.transpose(
                                        bank_bf(E_BANKS + n % 3)[:, (TPU * k + t) * P:(TPU * k + t + 1) * P],
                                        ASM[u % 2][:, t, f // 2, h:h + 2, :].rearrange("p h c -> p (h c)"), IDB[:, :])
                            last.then_inc(stacked, 1)

                    turn(0)
                    turn(1)
                    for b in range(NB):
                        project(2 * b)
                        project(2 * b + 1)
                        if b + 2 < NB:
                            turn(b + 2)
                    for u in range(NU):
                        stack(u)
                        for t in BESIDE.get(u, ()):
                            lead(0, t)
                    for t in BEHIND:
                        lead(0, t)
                    pe.wait_ge(stored, 4 * NU)
                    pe.wait_ge(m_kept, 2)
                    drive(pe, step)
                    for s in range(STEPS - LAG, STEPS):
                        product(NG - 1, s)
                    pe.wait_ge(normalised, NG * NB - 1)
                    pe.wait_ge(m_kept, NG * NB)
                    turn_output(NG - 1, NB - 1)

                @block.vector
                def _(dve):
                    def reduce(g, t):
                        b, c, q, w = max_step(t)
                        if t == FIRST[b]:
                            wait_for(dve, nm_ready, g * NB + b)
                        for pair in range(2):
                            wait_for(dve, s_full, g * (2 * STEPS) + (2 * t + pair + 1))
                            dve.tensor_reduce(MX[:, c, q, 2 * pair:2 * pair + 2],
                                              PS[:, S_BANKS + 2 * pair:S_BANKS + 2 * pair + 2, 0:w], AX.X, ALU.max)\
                               .then_inc(s_read, 1)
                        if t in M_END:
                            wait_for(dve, s_read, g * (2 * STEPS) + 2 * (t + 1))
                            wait_for(dve, mp_ready, g * NB + b)
                            dve.tensor_reduce(NM[:, :], MX[:, 0:b + 1, :, :].rearrange("p c q j -> p (q j) c"),
                                              AX.X, ALU.max, negate=True).then_inc(nm_ready, 1)

                    def keep_max(g, b):
                        wait_for(dve, m_turned, g * NB + (b + 1))
                        before = g * 64 + (64 if b >= 2 else 0)
                        wait_for(dve, m_written[(b - 2) % NB], before)
                        dve.tensor_copy(MT[:, b % 2, :], bank_bf(max_bank(g, b))[0:3 * HG, 0:BLK]).then_inc(m_kept, 1)

                    def normalise(g, b):
                        wait_for(dve, o_turned, g * NB + (b + 1))
                        o = bank(out_bank(b)).rearrange("p (q j c) -> p q j c", q=TPB, j=HG)
                        dve.reciprocal(RD[:, :, :], o[:, :, :, DH]).then_inc(recip, 1)
                        wait_for(dve, recip, g * NB + (b + 1))
                        dst = ATT[:, TPB * b:TPB * (b + 1), bass.ds(g * (HG * DH), HG * DH)]
                        dve.tensor_tensor(dst.rearrange("p q (j d) -> p q j d", d=DH), o[:, :, :, 0:DH],
                                          RD[:, :, :].unsqueeze(3).broadcast_to([P, TPB, HG, DH]), ALU.mult)\
                           .then_inc(normalised, 1)

                    def lead(g, t):
                        reduce(g, t)
                        if t - M_TURN in M_END:
                            keep_max(g, M_END[t - M_TURN])

                    def step(g, s, prev, nxt):
                        if at := beside(g, s, nxt):
                            reduce(*at)
                        if at := maxima_ended(g, s, nxt, M_TURN):
                            keep_max(*at)
                        if at := block_ended(g, s, prev, O_TURN):
                            normalise(*at)

                    def rotate(u):
                        dve.wait_ge(qk_kept, u + 1)
                        x1, x2 = (QK[:, u].rearrange("p t a (m two) -> p t a m two", two=2)[:, :, :, :, n] for n in (0, 1))
                        y1, y2 = (ROT[u % 2].rearrange("p t a (m two) -> p t a m two", two=2)[:, :, :, :, n] for n in (0, 1))
                        cos, sin = (v[:, layer, TPU * u:TPU * (u + 1), :].unsqueeze(2).broadcast_to([P, TPU, 2, D // 2])
                                    for v in (COS, SIN))
                        if u >= 1:
                            dve.wait_ge(rotated, u)
                        dve.tensor_tensor(tmp[0], x1, cos, ALU.mult)
                        dve.tensor_tensor(tmp[1], x2, sin, ALU.mult)
                        dve.tensor_tensor(tmp[2], x1, sin, ALU.mult)
                        link(dve.tensor_tensor(tmp[3], x2, cos, ALU.mult))
                        dve.tensor_tensor(y1, tmp[0], tmp[1], ALU.subtract)
                        dve.tensor_tensor(y2, tmp[2], tmp[3], ALU.add).then_inc(rotated, 1)

                    link = Chain(dve, chain)
                    for b in range(NB):
                        row_statistics(dve, link, b, var_ready)
                        if b >= 1:
                            normalise_rows(dve, link, b - 1, root_ready).then_inc(normed, 1)
                    normalise_rows(dve, link, NB - 1, root_ready).then_inc(normed, 1)
                    rotate(0)
                    for u in range(NU):
                        dve.wait_ge(high, u + 1)
                        dve.tensor_tensor(rows_of(R1), rot_rows(u), asm_rows(u, 0), ALU.subtract).then_inc(rest1, 1)
                        if u + 1 < NU:
                            rotate(u + 1)
                        dve.wait_ge(mid, u + 1)
                        if u >= 1:
                            dve.wait_ge(low, u)
                        dve.tensor_tensor(rows_of(R2), rows_of(R1), asm_rows(u, 3), ALU.subtract).then_inc(rest2, 1)
                        for t in BESIDE.get(u - 1, ()):
                            lead(0, t)
                    for t in (*BESIDE[NU - 1], *BEHIND):
                        lead(0, t)
                    drive(dve, step)
                    normalise(NG - 1, NB - 1)

                @block.scalar
                def _(act):
                    def keep_output(g, b):
                        wait_for(act, pv_done, g * STEPS + FIRST[b + 1])
                        wait_for(act, o_turned, g * NB + b)
                        act.activation(OT[:, :], bank(O_BANK), ACT.Copy).then_inc(o_kept, 1)

                    def step(g, s, prev, nxt):
                        b, kt, q0 = exp_step(s)
                        wait_for(act, pv_done, g * STEPS + (s - NSLOT // HG + 1))
                        for j in range(HG):
                            e = 4 * s + j
                            wait_for(act, e_full, g * (4 * STEPS) + (e + 1))
                            act.activation(PR[:, e % NSLOT, 0:BLK - q0], PS[:, turning_bank(s, "exp", j), 0:BLK - q0],
                                           ACT.Exp, scale=SCALE).then_inc(e_done, 1)
                            if j == 1 and (at := block_ended(g, s, prev, O_KEEP)):
                                keep_output(*at)

                    def keep_turned(b):
                        act.wait_ge(turned, b + 1)
                        act.activation(XNT[:, BLK * b:BLK * (b + 1)], bank(O_BANK + b % 2), ACT.Copy).then_inc(kept, 1)

                    def keep_qkv(u):
                        act.wait_ge(qkv_ready, u + 1)
                        banks = slice(TPU * (u % 2), TPU * (u % 2) + TPU)
                        act.activation(QK[:, u].rearrange("p t a n -> p t (a n)"), PS[:, banks, 0:2 * D], ACT.Copy)\
                           .then_inc(qk_kept, 1)
                        act.activation(VX[:, TPU * u:TPU * (u + 1), :, 0:DH],
                                       PS[:, banks, 2 * D:3 * D].rearrange("p t (h d) -> p t h d", d=DH), ACT.Copy)\
                           .then_inc(v_kept, 1)

                    def store(n):
                        u, f = divmod(n, 4)
                        act.wait_ge(stacked, n + 1)
                        dst = (QA, KA)[f // 2][:, 4 * (f % 2):4 * (f % 2) + 4, TPU * P * u:TPU * P * (u + 1)].bitcast(I32)
                        act.copy(dst, PS[:, E_BANKS + n % 3, :].bitcast(I32).rearrange("p (s n) -> p s n", s=4))\
                           .then_inc(stored, 1)

                    for b in range(NB):
                        root(act, b, var_ready, root_ready)
                    keep_turned(0)
                    keep_turned(1)
                    for b in range(NB):
                        keep_qkv(2 * b)
                        keep_qkv(2 * b + 1)
                        if b + 2 < NB:
                            keep_turned(b + 2)
                    for u in range(NU):
                        act.wait_ge(rotated, u + 1)
                        if u >= 2:
                            act.wait_ge(stacked, 4 * (u - 1))
                        act.activation(asm_rows(u, 0), rot_rows(u), ACT.Copy).then_inc(high, 1)
                        if u >= 1:
                            store(4 * (u - 1))
                            store(4 * (u - 1) + 1)
                        act.wait_ge(rest1, u + 1)
                        act.activation(asm_rows(u, 3), rows_of(R1), ACT.Copy).then_inc(mid, 1)
                        if u >= 1:
                            store(4 * (u - 1) + 2)
                            store(4 * (u - 1) + 3)
                        act.wait_ge(rest2, u + 1)
                        r2 = R2.rearrange("p (t a h d) -> p t a h d", t=TPU, a=2, h=H)
                        act.activation(part(u, 0, 5), r2[:, :, 0], ACT.Copy)
                        act.activation(part(u, 1, 4), r2[:, :, 1], ACT.Copy).then_inc(low, 1)
                    for f in range(4):
                        store(4 * (NU - 1) + f)
                    drive(act, step)
                    keep_output(NG - 1, NB - 1)

                @block.gpsimd
                def _(pool):
                    def load_v(g, b):
                        tiles = slice(TPB * b, TPB * (b + 1))
                        pool.tensor_copy(VG[:, tiles, :, 0:DH + 1], VX[:, tiles, bass.ds(g * HG, HG), :]).then_inc(v_loaded, 1)

                    def split_max(g, b):
                        wait_for(pool, nm_ready, g * NB + (b + 1))
                        wait_for(pool, m_turned, g * NB + b)
                        mp = MP[:, :, :, :].rearrange("p q j n -> p (q j) n")
                        pool.tensor_copy(mp[:, :, 0], NM[:, :]).then_inc(nm_chain, 1)
                        wait_for(pool, nm_chain, g * (4 * NB) + (4 * b + 1))
                        pool.tensor_tensor(NR[:, 0, :], NM[:, :], mp[:, :, 0], ALU.subtract).then_inc(nm_chain, 1)
                        wait_for(pool, nm_chain, g * (4 * NB) + (4 * b + 2))
                        pool.tensor_copy(mp[:, :, 1], NR[:, 0, :]).then_inc(nm_chain, 1)
                        wait_for(pool, nm_chain, g * (4 * NB) + (4 * b + 3))
                        pool.tensor_tensor(NR[:, 1, :], NR[:, 0, :], mp[:, :, 1], ALU.subtract).then_inc(nm_chain, 1)
                        wait_for(pool, nm_chain, g * (4 * NB) + (4 * b + 4))
                        pool.tensor_copy(mp[:, :, 2], NR[:, 1, :]).then_inc(mp_ready, 1)

                    def lead(g, t):
                        if t in M_END:
                            split_max(g, M_END[t])

                    def step(g, s, prev, nxt):
                        b, kt, q0 = exp_step(s)
                        n = s - LAG - 1 - FIRST[NB - 1]
                        if n > 0 and n % TPB == 0 and nxt is not None:
                            wait_for(pool, pv_done, g * STEPS + (s - LAG - 1))
                            load_v(nxt, n // TPB - 1)
                        if s == LAG and prev is not None:
                            wait_for(pool, pv_done, g * STEPS)
                            load_v(g, NB - 1)
                        if kt >= TPB * b:
                            wait_for(pool, e_done, g * (4 * STEPS) + 4 * (s + 1))
                            v = PR[:, 4 * s % NSLOT:4 * s % NSLOT + HG, 0:P]
                            pool.affine_select(out=v, in_=v, compare_op=ALU.is_ge, fill=0.0, base=0,
                                               pattern=[[0, HG], [1, P]], channel_multiplier=-1).then_inc(masked, 1)
                        if at := maxima_ended(g, s, nxt, 0):
                            split_max(*at)

                    for n in range(2):
                        if n:
                            pool.wait_ge(qkv_ready, NU)
                        pool.memset(ASM[n][:, :, :, :, MROW:ROWS], 0.0).then_inc(edge, 1)
                        pool.wait_ge(edge, 2 * n + 1)
                        pool.memset(ASM[n][:, :, 1, :, MROW:MROW + 3], 1.0).then_inc(edge, 1)
                    for u in range(NU):
                        pool.wait_ge(high, u + 1)
                        pool.tensor_copy(part(u, 0, 1), part(u, 0, 0))
                        pool.tensor_copy(part(u, 0, 4), part(u, 0, 0))
                        pool.tensor_copy(part(u, 1, 2), part(u, 1, 0))
                        pool.tensor_copy(part(u, 1, 5), part(u, 1, 0))
                        pool.wait_ge(mid, u + 1)
                        pool.tensor_copy(part(u, 0, 2), part(u, 0, 3))
                        pool.tensor_copy(part(u, 1, 1), part(u, 1, 3)).then_inc(doubled, 1)
                        for t in BESIDE.get(u - 1, ()):
                            lead(0, t)
                    pool.wait_ge(v_kept, NU)
                    for b in range(NB):
                        load_v(0, b)
                    for t in (*BESIDE[NU - 1], *BEHIND):
                        lead(0, t)
                    drive(pool, step)

        def feed_forward(layer):
            L = f"l{layer}_"
            a_turned, a_kept, projected, added = (sem(L + n) for n in ("att_turned", "att_kept", "projected", "added"))
            normed, turned, kept = sem(L + "ff_normed"), sem(L + "ff_turned"), sem(L + "ff_kept")
            hid_full, hid_done, gate_done = sem(L + "hid_full"), sem(L + "hid_done"), sem(L + "gate_done")
            down, chain, stored = sem(L + "down"), sem(L + "ff_chain"), sem(L + "stored")
            var_ready, root_ready = sem(L + "ff_var"), sem(L + "ff_root")
            nh = (C0, C1)[layer]
            AT = work(0, T)
            HT = [work(2048 + 512 * n, 512) for n in range(2 * nh)]
            GT = [work(6144 + 512 * n, 512) for n in range(2)]

            with nc.Block() as block:
                def wo(pe, b):
                    pe.wait_ge(a_kept, b + 1)
                    if b >= 2:
                        pe.wait_ge(added, b - 1)
                    for t in range(TPB):
                        at = P * (TPB * b + t)
                        last = pe.matmul(PS[:, E_BANKS + b % 2, t * P:(t + 1) * P], AT[:, at:at + P], WO[:, layer, :],
                                         start=True, stop=True)
                    last.then_inc(projected, 1)

                def up(pe, b):
                    pe.wait_ge(kept, b + 1)
                    xs = XNT[:, BLK * b:BLK * (b + 1)]
                    for c in range(nh):
                        for k, w in enumerate((W1T,) if layer == 0 else (WGT, WUT)):
                            n = ((1, 2)[layer]) * (nh * b + c) + k
                            if n >= 4:
                                pe.wait_ge(hid_done if layer == 0 or k else gate_done,
                                           n - 3 if layer == 0 else (n - 4) // 2 + 1)
                            pe.matmul(bank(n % 4), w[:, c * P:(c + 1) * P], xs, start=True, stop=True).then_inc(hid_full, 1)

                def back(pe, b):
                    pe.wait_ge(hid_done, nh * (b + 1))
                    pe.wait_ge(added, NB)
                    if b >= 2:
                        pe.wait_ge(added, NB + b - 1)
                    w = (W2T, WDT)[layer]
                    for t in range(TPB):
                        for c in range(nh):
                            last = pe.matmul(PS[:, E_BANKS + b % 2, t * P:(t + 1) * P],
                                             HT[nh * (b % 2) + c][:, t * P:(t + 1) * P], w[:, c, :],
                                             start=(c == 0), stop=(c == nh - 1))
                    last.then_inc(down, 1)

                @block.tensor
                def _(pe):
                    for b in range(NB):
                        if b >= 2:
                            pe.wait_ge(a_kept, b - 1)
                        for t in range(TPB):
                            last = pe.transpose(PS[:, O_BANK + b % 2, t * P:(t + 1) * P], ATT[:, TPB * b + t, :], IDF[:, :])
                        last.then_inc(a_turned, 1)
                        if b >= 1:
                            wo(pe, b - 1)
                    wo(pe, NB - 1)
                    for b in range(NB):
                        pe.wait_ge(normed, b + 1)
                        pe.wait_ge(a_kept, NB)
                        if b >= 2:
                            pe.wait_ge(kept, b - 1)
                        for t in range(TPB):
                            last = pe.transpose(PS[:, O_BANK + b % 2, t * P:(t + 1) * P], XN[:, TPB * b + t, :], IDF[:, :])
                        last.then_inc(turned, 1)
                        up(pe, b)
                        if b >= 1:
                            back(pe, b - 1)
                    back(pe, NB - 1)

                @block.scalar
                def _(act):
                    for b in range(NB):
                        act.wait_ge(a_turned, b + 1)
                        act.activation(AT[:, BLK * b:BLK * (b + 1)], bank(O_BANK + b % 2), ACT.Copy).then_inc(a_kept, 1)
                    for b in range(NB):
                        root(act, b, var_ready, root_ready)
                    for b in range(NB):
                        act.wait_ge(turned, b + 1)
                        act.activation(XNT[:, BLK * b:BLK * (b + 1)], bank(O_BANK + b % 2), ACT.Copy).then_inc(kept, 1)
                        for c in range(nh):
                            n = nh * b + c
                            if layer == 0:
                                act.wait_ge(hid_full, n + 1)
                                if b >= 2:
                                    act.wait_ge(down, b - 1)
                                act.activation(HT[nh * (b % 2) + c], bank(n % 4), ACT.Gelu, bias=B1[:, c:c + 1])\
                                   .then_inc(hid_done, 1)
                            else:
                                act.wait_ge(hid_full, 2 * n + 1)
                                if n >= 2:
                                    act.wait_ge(hid_done, n - 1)
                                act.activation(GT[n % 2], bank(2 * n % 4), ACT.Silu).then_inc(gate_done, 1)

                def add(dve, link, b):
                    dve.wait_ge(down, b + 1)
                    x = X[:, TPB * b:TPB * (b + 1), :]
                    o = bank(E_BANKS + b % 2).rearrange("p (t d) -> p t d", t=TPB)
                    if layer == 0:
                        tmp = XN[:, TPB * b:TPB * (b + 1), :]
                        link(dve.tensor_tensor(tmp, o, B2[:, :].unsqueeze(1).broadcast_to([P, TPB, D]), ALU.add))
                        dve.tensor_tensor(x, x, tmp, ALU.add).then_inc(added, 1)
                    else:
                        dve.tensor_tensor(x, x, o, ALU.add).then_inc(added, 1)

                @block.vector
                def _(dve):
                    link = Chain(dve, chain)
                    for b in range(NB):
                        dve.wait_ge(projected, b + 1)
                        x = X[:, TPB * b:TPB * (b + 1), :].rearrange("p t d -> p (t d)")
                        dve.tensor_tensor(x, x, bank(E_BANKS + b % 2), ALU.add).then_inc(added, 1)
                        dve.wait_ge(added, b + 1)
                        dve.wait_ge(a_turned, b + 1)
                        row_statistics(dve, link, b, var_ready)
                        if b >= 1:
                            normalise_rows(dve, link, b - 1, root_ready).then_inc(normed, 1)
                    normalise_rows(dve, link, NB - 1, root_ready).then_inc(normed, 1)
                    for b in range(NB):
                        if layer == 1:
                            for c in range(nh):
                                n = nh * b + c
                                dve.wait_ge(gate_done, n + 1)
                                dve.wait_ge(hid_full, 2 * n + 2)
                                if b >= 2:
                                    dve.wait_ge(down, b - 1)
                                dve.tensor_tensor(HT[nh * (b % 2) + c], GT[n % 2], bank((2 * n + 1) % 4), ALU.mult)\
                                   .then_inc(hid_done, 1)
                            if b >= 1:
                                add(dve, link, b - 1)
                        else:
                            add(dve, link, b)
                    if layer == 1:
                        add(dve, link, NB - 1)

                @block.sync
                def _(sp):
                    if layer == 1:
                        for b in range(NB):
                            sp.wait_ge(added, NB + b + 1)
                            sp.dma_start(out[0, BLK * b:BLK * (b + 1), :].rearrange("(i p) d -> p i d", p=P),
                                         X[:, TPB * b:TPB * (b + 1), :]).then_inc(stored, 16)
                        sp.wait_ge(stored, 16 * NB)

        for layer in range(2):
            attention(layer)
            feed_forward(layer)


_INS = ['L0_attn_x', 'L0_attn_w_qkv', 'L0_attn_w_o', 'L0_attn_log_scale', 'L0_ffn_w1', 'L0_ffn_b1', 'L0_ffn_w2',
        'L0_ffn_b2', 'L1_attn_W_q', 'L1_attn_W_k', 'L1_attn_W_v', 'L1_attn_W_o', 'L1_ffn_w_gate', 'L1_ffn_w_up',
        'L1_ffn_w_down']


def kernel(**inputs):
    import numpy as _np
    import concourse.bacc as _bacc
    from concourse import mybir as _mybir
    from concourse.bass_utils import run_bass_kernel_spmd as _run

    nc = _bacc.Bacc("TRN2", target_bir_lowering=False, num_devices=1)
    arrays, args = {}, []
    for name in _INS:
        a = _np.ascontiguousarray(inputs[name])
        arrays[f"in_{name}"] = a
        args.append(nc.dram_tensor(f"in_{name}", a.shape, _mybir.dt.from_np(a.dtype), kind="ExternalInput").ap())
    args.append(nc.dram_tensor("out_x", (1, T, D), _mybir.dt.float32, kind="ExternalOutput").ap())
    build(nc, *args)
    r = _run(nc, [arrays], core_ids=[0])
    return r.results[0]["out_x"]
```

```python
from collections import namedtuple
from contextlib import ExitStack

import numpy as np

import concourse.bass as bass
from concourse import mybir

FP32, BF16, I32 = mybir.dt.float32, mybir.dt.bfloat16, mybir.dt.int32
ALU = mybir.AluOpType
ACT = mybir.ActivationFunctionType
AX = mybir.AxisListType

P = 128
T, D = 2048, 128
H, DH = 16, 8
NT = T // P
BLK = 512
TPB = BLK // P
NB = T // BLK
TPU = 2
NU = NT // TPU
HG = 4
NG = H // HG
ROWS = 64
MROW = 48
VW = 32
HID0, HID1 = 512, 384
C0, C1 = HID0 // P, HID1 // P
EPS = 1e-5
SCALE = float(DH) ** -0.5
NEG = -1e30

FIRST = [sum(TPB * (q + 1) for q in range(b)) for b in range(NB + 1)]
STEPS = FIRST[NB]
LEAD = 20
HEAD = STEPS - LEAD
LAG = 2
NSLOT = 16
S_BANKS, E_BANKS, O_BANK, X_BANK = 0, 4, 6, 7
AT_BANKS, WO_BANKS = (0, 1, 2, 4), (3, 3, 3, 5)
TURNING = (4, 5, 7)


def block_of(step):
    return max(b for b in range(NB) if FIRST[b] <= step)


def rope_frequencies():
    gamma = np.asarray((14.134725142, 21.022039639, 25.01085758, 30.424876126), np.float32)
    inv0 = np.float32(1.0) / (gamma / gamma[0])
    inv1 = np.float32(10000.0) ** (np.float32(-2.0) * np.arange(DH // 2, dtype=np.float32) / np.float32(DH))
    return [float(v) for v in inv0], [float(v) for v in inv1.astype(np.float32)]


def wait(eng, sem, value):
    eng.wait_ge(sem, value)
    eng.sem_inc(wait.passed, 1)


Programs = namedtuple("Programs", "sync tensor vector scalar gpsimd", defaults=(None,))


class Chain:

    def __init__(self, eng, sem):
        self.eng, self.sem, self.n = eng, sem, 0

    def __call__(self, ins):
        self.n += 1
        ins.then_inc(self.sem, 1)
        self.eng.wait_ge(self.sem, self.n)

    def mark(self, ins):
        self.n += 1
        ins.then_inc(self.sem, 1)
        return self.n


def build(nc, x_in, w_qkv, w_o0, log_scale, w1, b1, w2, b2, w_q, w_k, w_v, w_o1, w_gate, w_up, w_down, out):
    ctx = ExitStack()
    with ctx:
        def sb(name, shape, dt):
            return ctx.enter_context(nc.sbuf_tensor(name, shape, dt))

        def sem(name):
            return ctx.enter_context(nc.semaphore(name))

        X = sb("x_res", [P, NT, D], FP32)
        XN = sb("x_norm", [P, NT, D], FP32)
        ATT = XN
        VX = sb("v_all", [P, NT, H, DH + 1], FP32)
        QKA = sb("q_and_k_all", [P, 2, H // 2, T], BF16)
        QA, KA = QKA[:, 0], QKA[:, 1]
        Q2 = sb("q_group", [P, HG // 2, T], BF16)
        K2 = sb("k_group", [P, HG, T], BF16)
        QK1 = sb("q_and_k_group_max", [P, 2, T], BF16)
        VG = sb("v_group", [P, NT, HG, VW], FP32)
        WORK = sb("work", [P, 11264], FP32)
        SIN = sb("sin", [P, 2, NT, H * DH // 2], FP32)
        COS = sb("cos", [P, 2, NT, H * DH // 2], FP32)
        WQKV = sb("w_qkv_sb", [P, 2, 3 * D], FP32)
        WO = sb("w_o_sb", [P, 2, D], FP32)
        W1T = sb("w1_t", [P, HID0], FP32)
        W2T = sb("w2_t", [P, C0, D], FP32)
        WGT = sb("w_gate_t", [P, HID1], FP32)
        WUT = sb("w_up_t", [P, HID1], FP32)
        WDT = sb("w_down_t", [P, C1, D], FP32)
        B1 = sb("b1_sb", [P, C0], FP32)
        B2 = sb("b2_sb", [P, D], FP32)
        IDF = sb("ident_f", [P, P], FP32)
        IDB = sb("ident_b", [P, P], BF16)
        CM = sb("causal_b", [P, P], BF16)
        STAT = sb("ln_stat", [P, NT, 6], FP32)
        MV = sb("ln_mv", [P, NT, 2], FP32)
        VAR = sb("ln_var", [P, NT], FP32)
        ROOT = sb("ln_root", [P, NT], FP32)
        RSTD = sb("ln_rstd", [P, NT], FP32)
        MX = sb("max_parts", [P, NB, TPB, HG], FP32)
        NM = sb("neg_max", [P, TPB * HG], FP32)
        NR = sb("neg_max_rest", [P, 2, TPB * HG], FP32)
        MP = sb("neg_max_bf", [P, TPB, HG, 3], BF16)
        MT = sb("neg_max_rows", [HG * 3, 2, BLK], BF16)
        RD = sb("o_recip", [P, TPB, HG], FP32)

        PS = ctx.enter_context(nc.psum_tensor("ps", [P, 8, 512], FP32))

        def bank(n):
            return PS[:, n, :]

        def bank_bf(n):
            return PS[:, n, :].bitcast(BF16)

        def work(at, n):
            return WORK[:, at:at + n]

        PR = WORK[:, 0:NSLOT * BLK].rearrange("p (s n) -> p s n", s=NSLOT)

        OT = work(NSLOT * BLK, BLK)
        inv0, inv1 = rope_frequencies()

        ld_x = [sem(f"x_loaded{b}") for b in range(NB)]
        ld_qkv, ld_w, ld_b = sem("w_qkv_loaded"), sem("weights_loaded"), sem("biases_loaded")
        ident_ready, scale_ready, zeroed = sem("ident_ready"), sem("scale_ready"), sem("zeroed")
        wait.passed = sem("waits_passed")
        pool_chain, dve_chain = sem("setup_pool_chain"), sem("setup_dve_chain")
        turns_ready = sem("turns_ready")
        theta_ready, sin_ready, tables = sem("theta_ready"), sem("sin_ready"), sem("tables_ready")
        raw_ready, w_turned, w_kept = sem("raw_ready"), sem("w_turned"), sem("w_kept")

        normalised, att_normed, a_turned, a_kept, projected, added = (
            [sem(f"l{n}_{name}") for n in range(2)]
            for name in ("normalised", "normed", "att_turned", "att_kept", "projected", "added"))
        var_ready, root_ready = ([sem(f"ln{n}_{name}") for n in range(4)] for name in ("var", "root"))

        POSI = sb("positions_i", [P, NT], I32)
        POSF = sb("positions_f", [P, NT], FP32)
        TH0 = sb("angles_unscaled", [P, NT, DH // 2], FP32)
        ESC = sb("exp_log_scale", [P, H], FP32)
        AL = sb("mean_abs", [P, 2, C0], FP32)
        SG1, SG2 = SIN[:, 1].rearrange("p i m -> p (i m)")[:, 0:512], COS[:, 1].rearrange("p i m -> p (i m)")[:, 0:512]
        WI = [w.rearrange("p (c n) -> p c n", c=C1) for w in (WGT[:, :], WUT[:, :])] + [WDT[:, :, :]]
        TURNED = [[WQKV[:, 1, n * P:(n + 1) * P] for n in range(3)] + [WO[:, 1, :]],
                  [W1T[:, n * P:(n + 1) * P] for n in range(C0)], [W2T[:, n, :] for n in range(C0)],
                  *[[w[:, n, :] for n in range(C1)] for w in WI]]

        def load_inputs(sp):
            for b in range(NB):
                sp.dma_start(X[:, TPB * b:TPB * (b + 1), :],
                             x_in[0, BLK * b:BLK * (b + 1), :].rearrange("(i p) d -> p i d", p=P)).then_inc(ld_x[b], 16)
                if b == 0:
                    sp.dma_start(WQKV[:, 0, :], w_qkv).then_inc(ld_qkv, 16)
            sp.dma_start(W1T[:, :].rearrange("p (c d) -> p c d", c=C0),
                         w1.rearrange("(c p) d -> p c d", p=P)).then_inc(ld_w, 16)
            sp.dma_start(W2T[:, :, :], w2.rearrange("p (c n) -> p c n", c=C0)).then_inc(ld_w, 16)
            for n, w in enumerate((w_gate, w_up)):
                sp.dma_start(WI[n].bitcast(I32), w.rearrange("(c p) d -> p c d", p=P)).then_inc(ld_w, 16)
            sp.dma_start(WI[2].bitcast(I32), w_down.rearrange("p (c n) -> p c n", c=C1)).then_inc(ld_w, 16)
            for n, w in enumerate((w_q, w_k, w_v, w_o1)):
                sp.dma_start(TURNED[0][n], w).then_inc(ld_w, 16)
            sp.dma_start(WO[:, 0, :], w_o0).then_inc(ld_w, 16)

        def load_biases(act):
            act.dma_start(ESC[:, :], log_scale.rearrange("(a n) -> a n", a=1).broadcast_to([P, H])).then_inc(ld_b, 16)
            act.wait_ge(ld_b, 16)
            act.activation(ESC[:, :], ESC[:, :], ACT.Exp).then_inc(scale_ready, 1)
            act.dma_start(B1[:, :], b1.rearrange("(c p) -> p c", p=P), allow_slow_non_contiguous=True).then_inc(ld_b, 16)
            act.dma_start(B2[:, :], b2.rearrange("(a n) -> a n", a=1).broadcast_to([P, D])).then_inc(ld_b, 16)

        def constants(pool):
            pool.iota(POSI[:, :], pattern=[[P, NT]], base=0, channel_multiplier=1).then_inc(pool_chain, 1)
            for m in (IDF, IDB, CM):
                pool.memset(m[:, :], 0.0).then_inc(pool_chain, 1)
            pool.wait_ge(pool_chain, 4)
            for m in (IDF, IDB):
                pool.affine_select(out=m[:, :], in_=m[:, :], compare_op=ALU.not_equal, fill=1.0,
                                   base=0, pattern=[[-1, P]], channel_multiplier=1).then_inc(ident_ready, 1)
            pool.affine_select(out=CM[:, :], in_=CM[:, :], compare_op=ALU.is_ge, fill=NEG,
                               base=0, pattern=[[-1, P]], channel_multiplier=1).then_inc(ident_ready, 1)

        def angles(eng, link, layer):
            th, k = (v[:, layer].rearrange("p i m -> p (i m)") for v in (SIN, COS))
            if layer == 0:
                link(eng.tensor_copy(POSF[:, :], POSI[:, :]))
            for f in range(DH // 2):
                ins = eng.tensor_scalar(TH0[:, :, f], POSF[:, :], (inv0, inv1)[layer][f], None, ALU.mult)
                last = link.mark(ins)
            eng.wait_ge(link.sem, last)
            th4 = th.rearrange("p (i h f) -> p i h f", i=NT, h=H)
            t0 = TH0[:, :, :].unsqueeze(2).broadcast_to([P, NT, H, DH // 2])
            if layer == 0:
                eng.wait_ge(scale_ready, 1)
                e = ESC[:, :].unsqueeze(1).unsqueeze(3).broadcast_to([P, NT, H, DH // 2])
                link(eng.tensor_tensor(th4, t0, e, ALU.mult))
            else:
                link(eng.tensor_copy(th4, t0))
            magic = 1.5 * 2.0 ** 23
            link(eng.tensor_scalar(k, th, float(1 / (2 * np.pi)), magic, ALU.mult, ALU.add))
            eng.tensor_scalar(k, k, magic, None, ALU.subtract).then_inc(turns_ready, 1)

        def reduce_angles(dve, link, layer):
            th, k = (v[:, layer].rearrange("p i m -> p (i m)") for v in (SIN, COS))
            dve.wait_ge(turns_ready, layer + 1)
            c1 = 6.28125
            c2 = float(np.float32(np.round((2 * np.pi - c1) * 2 ** 21) / 2 ** 21))
            c3 = float(np.float32(2 * np.pi - c1 - c2))
            for c in (c1, c2, c3):
                link(dve.scalar_tensor_tensor(out=th, in0=k, scalar=-c, in1=th, op0=ALU.mult, op1=ALU.add))
            dve.tensor_scalar(th, th, 3.1415925, -3.1415925, ALU.min, ALU.max).then_inc(theta_ready, 1)

        def sines(act, layer):
            th, k = (v[:, layer].rearrange("p i m -> p (i m)") for v in (SIN, COS))
            act.wait_ge(theta_ready, layer + 1)
            act.activation(k, th, ACT.Sin, scale=0.5).then_inc(sin_ready, 1)
            act.activation(th, th, ACT.Sin).then_inc(sin_ready, 1)

        def cosines(eng, link, layer):
            k = COS[:, layer].rearrange("p i m -> p (i m)")
            eng.wait_ge(sin_ready, 2 * layer + 2)
            link(eng.tensor_tensor(k, k, k, ALU.mult))
            eng.tensor_scalar(k, k, -2.0, 1.0, ALU.mult, ALU.add).then_inc(tables, 1)

        def prepare_weights(dve, link):
            dve.wait_ge(ld_w, 16 * 10)
            for w in WI:
                link(dve.tensor_scalar(w, w.bitcast(I32), float(np.float32(1.0 / 127.0)), None, ALU.mult))
            for n, (s, red) in enumerate(((W1T[:, :].rearrange("p (c n) -> p c n", c=C0), P),
                                          (W2T[:, :, :].rearrange("p c n -> p (c n)").unsqueeze(1), HID0))):
                c = s.shape[1]
                al = AL[:, n, 0:c]
                g1 = SG1.rearrange("p (c n) -> p c n", c=c)
                g2 = SG2.rearrange("p (c n) -> p c n", c=c)
                link(dve.tensor_reduce(al, s, AX.X, ALU.add, apply_absolute_value=True))
                link(dve.tensor_scalar(al, al, 1.0 / red, None, ALU.mult))
                link(dve.tensor_scalar(g1, s, 0.0, None, ALU.is_gt))
                link(dve.tensor_scalar(g2, s, 0.0, None, ALU.is_lt))
                link(dve.tensor_tensor(g1, g1, g2, ALU.subtract))
                link(dve.tensor_tensor(g1, g1, al.unsqueeze(2).broadcast_to([P, c, 512 // c]), ALU.mult))
                link(dve.tensor_tensor(g1, g1, s, ALU.subtract))
                link(dve.tensor_tensor(s, s, g1, ALU.add))
            dve.sem_inc(raw_ready, 1)

        def turn_weights(pe, n):
            pe.wait_ge(ld_w, 16 * 10)
            if n >= 1:
                pe.wait_ge(raw_ready, 1)
            if n >= 4:
                pe.wait_ge(w_kept, n - 3)
            for c, src in enumerate(TURNED[n]):
                last = pe.transpose(PS[:, n % 4, c * P:(c + 1) * P], src, IDF[:, :])
            last.then_inc(w_turned, 1)

        def keep_weights(dve, n):
            dve.wait_ge(w_turned, n + 1)
            if n == 0:
                dve.tensor_copy(WQKV[:, 1, :], PS[:, 0, 0:3 * D])
                dve.tensor_copy(WO[:, 1, :], PS[:, 0, 3 * D:4 * D]).then_inc(w_kept, 1)
            else:
                dst = (W1T[:, :], W2T[:, :, :].rearrange("p c n -> p (c n)"), WGT[:, :], WUT[:, :],
                       WDT[:, :, :].rearrange("p c n -> p (c n)"))[n - 1]
                dve.tensor_copy(dst, PS[:, n % 4, 0:dst.shape[1]]).then_inc(w_kept, 1)

        def row_statistics(dve, link, blocks, var_ready, loaded=None):
            ts = slice(TPB * blocks[0], TPB * (blocks[-1] + 1))
            for b in blocks:
                if loaded:
                    dve.wait_ge(loaded[b], 16)
                for i in range(TPB * b, TPB * (b + 1)):
                    n = link.mark(dve.bn_stats(STAT[:, i, :], X[:, i, :]))
            dve.wait_ge(link.sem, n)
            for i in range(ts.start, ts.stop):
                m = link.mark(dve.bn_aggr(MV[:, i, :], STAT[:, i, :]))
            dve.wait_ge(link.sem, m)
            dve.tensor_scalar(VAR[:, ts], MV[:, ts, 1], EPS, None, ALU.add).then_inc(var_ready, 1)

        def root(act, n, blocks, var_ready, root_ready):
            ts = slice(TPB * blocks[0], TPB * (blocks[-1] + 1))
            act.wait_ge(var_ready, n)
            act.activation(ROOT[:, ts], VAR[:, ts], ACT.Sqrt).then_inc(root_ready, 1)

        def invert_roots(dve, link, n, blocks, root_ready):
            ts = slice(TPB * blocks[0], TPB * (blocks[-1] + 1))
            dve.wait_ge(root_ready, n)
            link(dve.reciprocal(RSTD[:, ts], ROOT[:, ts]))
            link(dve.tensor_tensor(ROOT[:, ts], RSTD[:, ts], RSTD[:, ts], ALU.mult))
            link(dve.tensor_tensor(ROOT[:, ts], ROOT[:, ts], VAR[:, ts], ALU.mult))
            link(dve.tensor_scalar(ROOT[:, ts], ROOT[:, ts], -0.5, 1.5, ALU.mult, ALU.add))
            link(dve.tensor_tensor(RSTD[:, ts], RSTD[:, ts], ROOT[:, ts], ALU.mult))

        def normalise_rows(dve, b):
            for i in range(TPB * b, TPB * (b + 1)):
                last = dve.tensor_scalar(XN[:, i, :], X[:, i, :], MV[:, i, 0:1], RSTD[:, i:i + 1],
                                         ALU.subtract, ALU.mult)
            return last

        def attention(layer):
            L = f"l{layer}_"
            p1_loaded = [sem(f"{L}max_operands{b}") for b in range(NB)]
            p2_loaded = [sem(f"{L}operands{b}") for b in range(NB)]
            m_written = [sem(f"{L}max_rows{b}") for b in range(NB)]
            v_loaded = sem(L + "v_group")
            s_full, s_read = sem(L + "scores_full"), sem(L + "scores_read")
            nm_ready, nm_chain, mp_ready = sem(L + "neg_max"), sem(L + "split_chain"), sem(L + "max_split")
            m_turned, m_kept = sem(L + "max_turned"), sem(L + "max_kept")
            e_full, e_done, masked = sem(L + "exp_in"), sem(L + "exp_done"), sem(L + "masked")
            pv_done, o_kept, o_turned = sem(L + "pv_done"), sem(L + "o_kept"), sem(L + "o_turned")
            recip, o_ready, normed = sem(L + "recip"), normalised[layer], att_normed[layer]
            turned, kept = sem(L + "xn_turned"), sem(L + "xn_kept")
            qkv_ready, qk_kept, v_kept = sem(L + "qkv_ready"), sem(L + "qk_kept"), sem(L + "v_kept")
            chain, rotated, rest1, rest2 = sem(L + "op_chain"), sem(L + "rotated"), sem(L + "rest1"), sem(L + "rest2")
            high, mid, low, doubled = sem(L + "high"), sem(L + "mid"), sem(L + "low"), sem(L + "doubled")
            edge, stacked, stored = sem(L + "edge"), sem(L + "stacked"), sem(L + "stacks_stored")

            QK = work(0, NU * 512).rearrange("p (u t a n) -> p u t a n", u=NU, t=TPU, a=2)
            ROT = [work(4096 + 512 * n, 512) for n in range(2)]
            tmp = [work(5120 + 256 * n, 256).rearrange("p (a t m) -> p t a m", t=TPU, a=2) for n in range(4)]
            R1, R2 = work(6144, 512), work(6656, 512)
            ASM = [work(7168 + 2048 * n, 2048).bitcast(BF16).rearrange("p (a t h c) -> p a t h c", t=TPU, a=2, h=H)
                   for n in range(2)]
            XNV = VG[:, :, :, :].rearrange("p i j c -> p (i j c)")

            def rows_of(v):
                return v.rearrange("p (r d) -> p r d", d=DH)

            def asm_rows(u, n):
                return ASM[u % 2].rearrange("p a t h c -> p (a t h) c")[:, :, DH * n:DH * (n + 1)]

            def part(u, a, n):
                return ASM[u % 2][:, a].rearrange("p t h c -> p (t h) c")[:, :, DH * n:DH * (n + 1)]

            def words(u, a):
                return ASM[u % 2][:, a].rearrange("p t h c -> p (t h) c").bitcast(I32)\
                    .rearrange("p r (n w) -> p r n w", w=DH // 2)

            BESIDE = {2: range(0, 1), 3: range(1, 3), 4: range(3, 4), 5: range(4, 6), 6: range(6, 8), 7: range(8, 12)}
            BEHIND = range(12, LEAD)

            M_END = {FIRST[b + 1] - 1: b for b in range(NB)}
            PREPARE = 22
            TURN_WEIGHTS = {23: (0,), 28: (1, 2, 3), 29: (4, 5)}
            TURN_ATT, PROJECT_ATT = {31: 0, 33: 1, 35: 2}, {32: 0, 34: 1, 36: 2}
            M_TURN, O_TURN, O_KEEP = 2, 4, 2

            def max_step(t):
                b = block_of(t)
                c, q = divmod(t - FIRST[b], TPB)
                return b, c, q, (BLK if c < b else P * (q + 1))

            def exp_step(s):
                b = block_of(s)
                kt = s - FIRST[b]
                return b, kt, P * max(0, kt - TPB * b)

            def beside(g, s, nxt):
                return (g, s + LEAD) if s < HEAD else (nxt, s - HEAD) if nxt is not None else None

            def maxima_ended(g, s, nxt, ago):
                t = s + LEAD - ago
                who, t = (g, t) if t < STEPS else (nxt, t - STEPS)
                return (who, M_END[t]) if t in M_END and who is not None else None

            def block_ended(g, s, prev, ago):
                t = s - ago
                who, t = (g, t) if t >= 0 else (prev, t + STEPS)
                return (who, M_END[t]) if t in M_END and who is not None else None

            def drive(eng, step):
                for s in range(HEAD):
                    step(0, s, None, None)
                with eng.Fori(0, NG - 1) as g:
                    for s in range(HEAD, STEPS):
                        step(g, s, None, g + 1)
                    for s in range(HEAD):
                        step(g + 1, s, g, None)
                for s in range(HEAD, STEPS):
                    step(NG - 1, s, None, None)

            def wait_for(eng, sem, value):
                if not (isinstance(value, int) and value <= 0):
                    if eng.engine in (mybir.EngineType.Pool, mybir.EngineType.SP):
                        wait(eng, sem, value)
                    else:
                        eng.wait_ge(sem, value)

            USES = []
            for s in range(STEPS):
                USES += [(s, "exp", j) for j in range(HG)]
                USES += [(s, "max", M_END[e]) for e in M_END if (e - LEAD + M_TURN - s) % STEPS == 0]
                USES += [(s, "out", M_END[e]) for e in M_END if (e + O_TURN - s) % STEPS == 0]
            assert len(USES) % len(TURNING) == 0

            def turning_bank(s, kind, n):
                return TURNING[USES.index((s % STEPS, kind, n)) % len(TURNING)]

            def max_bank(g, b):
                at = FIRST[b + 1] - 1 - LEAD + M_TURN
                return X_BANK if isinstance(g, int) and g == 0 and at < 0 else turning_bank(at, "max", b)

            def out_bank(b):
                return turning_bank(FIRST[b + 1] - 1 + O_TURN, "out", b)

            def bank_free(g, s, kind, n, prev):
                at = USES.index((s, kind, n)) - len(TURNING)
                while True:
                    if at < 0 and prev is None:
                        return e_done, 0
                    s, kind, n = USES[at % len(USES)]
                    before = 0 if at >= 0 else -1
                    if kind == "exp":
                        return e_done, g * (4 * STEPS) + (before * 4 * STEPS + 4 * s + n + 1)
                    if kind == "max":
                        ahead = 1 if s >= HEAD + M_TURN else 0
                        if not (isinstance(g, int) and g + before + ahead == NG):
                            return m_kept, g * NB + ((before + ahead) * NB + n + 1)
                    if kind == "out":
                        behind = 1 if s < O_TURN else 0
                        if not (isinstance(g, int) and g + before - behind < 0):
                            return o_ready, g * NB + ((before - behind) * NB + n + 1)
                    at -= len(TURNING)

            def sync(sp):
                if layer == 0:
                    load_inputs(sp)

                def load_max(g, b):
                    cols = slice(BLK * b, BLK * (b + 1))
                    for j in range(HG):
                        rows = slice(ROWS * (j % 2), ROWS * (j % 2) + 32)
                        sp.dma_start(QK1[32 * j:32 * j + 32, :, cols],
                                     QKA[rows, :, bass.ds(g * 2 + j // 2, 1), cols].squeeze(2)).then_inc(p1_loaded[b], 16)

                def load_exp(g, b):
                    cols = slice(BLK * b, BLK * (b + 1))
                    for j in range(2):
                        rows = slice(ROWS * j, ROWS * (j + 1))
                        sp.dma_start(K2[rows, j:HG:2, cols], KA[rows, bass.ds(g * 2, 2), cols]).then_inc(p2_loaded[b], 16)
                    sp.dma_start(Q2[:, :, cols], QA[:, bass.ds(g * 2, 2), cols]).then_inc(p2_loaded[b], 16)

                def write_max(g, b):
                    wait_for(sp, m_kept, g * NB + (b + 1))
                    wait_for(sp, p2_loaded[b], g * 48 + 48)
                    for j in range(HG):
                        at = ROWS * (j % 2) + MROW
                        sp.dma_start(Q2[at:at + 3, j // 2, BLK * b:BLK * (b + 1)], MT[3 * j:3 * j + 3, b % 2, :])\
                          .then_inc(m_written[b], 16)

                for b in range(NB):
                    sp.wait_ge(stored, 8 * (b + 1))
                    load_max(0, b)
                    if b == NB - 1:
                        write_max(0, 0)
                    sp.wait_ge(zeroed, 1)
                    load_exp(0, b)
                write_max(0, 1)
                with sp.Fori(0, NG - 1) as g:
                    write_max(g, 2)
                    for b in range(NB):
                        wait_for(sp, s_full, g * (2 * STEPS) + 2 * (FIRST[NB - 1] + TPB * (b + 1)))
                        load_max(g + 1, b)
                    write_max(g, 3)
                    for b in range(NB):
                        wait_for(sp, e_full, g * (4 * STEPS) + 4 * (FIRST[NB - 1] + TPB * (b + 1)))
                        load_exp(g + 1, b)
                        if b < 2:
                            write_max(g + 1, b)
                write_max(NG - 1, 2)
                write_max(NG - 1, 3)
                for b in range(NB):
                    sp.wait_ge(p1_loaded[b], 64 * NG)
                    sp.wait_ge(p2_loaded[b], 48 * NG)
                    sp.wait_ge(m_written[b], 64 * NG)

            def tensor(pe):
                def maxima(g, t, pairs=(0, 1)):
                    b, c, q, w = max_step(t)
                    if t == FIRST[b] and 0 in pairs:
                        wait_for(pe, p1_loaded[b], g * 64 + 64)
                    at = P * (TPB * b + q)
                    for pair in pairs:
                        wait_for(pe, s_read, g * (2 * STEPS) + (2 * t + pair - 1))
                        for j in (2 * pair, 2 * pair + 1):
                            rows = slice(32 * j, 32 * j + 32)
                            last = pe.matmul(PS[:, S_BANKS + j, 0:w], QK1[rows, 0, at:at + P],
                                             QK1[rows, 1, BLK * c:BLK * c + w], start=True, stop=(c < b))
                        if c == b:
                            for j in (2 * pair, 2 * pair + 1):
                                last = pe.matmul(PS[:, S_BANKS + j, w - P:w], IDB[:, :], CM[:, :],
                                                 start=False, stop=True)
                        last.then_inc(s_full, 1)

                def turn_max(g, b, at=None):
                    wait_for(pe, mp_ready, g * NB + (b + 1))
                    if at is None:
                        wait_for(pe, m_kept, b)
                    else:
                        wait_for(pe, *bank_free(*at))
                    for q in range(TPB):
                        last = pe.transpose(bank_bf(max_bank(g, b))[0:3 * HG, q * P:(q + 1) * P],
                                            MP[:, q, :, :].rearrange("p j n -> p (j n)"), IDB[:, :])
                    last.then_inc(m_turned, 1)

                def scores(g, s, j, prev):
                    b, kt, q0 = exp_step(s)
                    if kt == 0 and j == 0:
                        wait_for(pe, p2_loaded[b], g * 48 + 48)
                        wait_for(pe, m_written[b], g * 64 + 64)
                    wait_for(pe, *bank_free(g, s, "exp", j, prev))
                    pe.matmul(PS[:, turning_bank(s, "exp", j), 0:BLK - q0], K2[:, j, kt * P:(kt + 1) * P],
                              Q2[:, j // 2, BLK * b + q0:BLK * (b + 1)], start=True, stop=True).then_inc(e_full, 1)

                def product(g, s):
                    b, kt, q0 = exp_step(s)
                    if kt == 0:
                        wait_for(pe, o_kept, g * NB + b)
                        wait_for(pe, v_loaded, g * NB + (b + 1))
                    wait_for(pe, e_done, g * (4 * STEPS) + 4 * (s + 1))
                    if kt >= TPB * b:
                        wait_for(pe, masked, g * NT + (kt + 1))
                    for j in range(HG):
                        last = pe.matmul(PS[VW * j:VW * (j + 1), O_BANK, q0:BLK], VG[:, kt, j, :],
                                         PR[:, (4 * s + j) % NSLOT, 0:BLK - q0],
                                         start=(kt == 0), stop=(kt == TPB * (b + 1) - 1))
                    last.then_inc(pv_done, 1)

                def turn_output(g, b, at=None):
                    wait_for(pe, o_kept, g * NB + (b + 1))
                    if at is not None:
                        wait_for(pe, *bank_free(*at))
                    for q in range(TPB):
                        last = pe.transpose(PS[:, out_bank(b), q * P:(q + 1) * P], OT[:, q * P:(q + 1) * P], IDF[:, :])
                    last.then_inc(o_turned, 1)

                def lead(g, t):
                    maxima(g, t)
                    if t - M_TURN in M_END:
                        turn_max(g, M_END[t - M_TURN])

                def step(g, s, prev, nxt):
                    at = beside(g, s, nxt)
                    scores(g, s, 0, prev)
                    if at:
                        maxima(*at, (0,))
                    scores(g, s, 1, prev)
                    if s >= LAG:
                        product(g, s - LAG)
                    elif prev is not None:
                        product(prev, STEPS + s - LAG)
                    scores(g, s, 2, prev)
                    if at:
                        maxima(*at, (1,))
                    scores(g, s, 3, prev)
                    if who := maxima_ended(g, s, nxt, M_TURN):
                        turn_max(*who, (g, s, "max", who[1], prev))
                    if who := block_ended(g, s, prev, O_TURN):
                        turn_output(*who, (g, s, "out", who[1], prev))
                    if isinstance(g, int) and g == NG - 1 and s >= HEAD:
                        if s == PREPARE:
                            pe.wait_ge(s_read, NG * 2 * STEPS)
                        if layer == 0:
                            for n in TURN_WEIGHTS.get(s, ()):
                                turn_weights(pe, n)
                        if s in TURN_ATT:
                            pe.wait_ge(w_kept, len(TURNED))
                            turn_attention(pe, layer, TURN_ATT[s])
                        if s in PROJECT_ATT:
                            project_attention(pe, layer, PROJECT_ATT[s])

                def turn(b):
                    pe.wait_ge(normed, b + 1)
                    if b >= 2:
                        pe.wait_ge(kept, b - 1)
                    for t in range(TPB):
                        last = pe.transpose(PS[:, O_BANK + b % 2, t * P:(t + 1) * P], XN[:, TPB * b + t, :], IDF[:, :])
                    last.then_inc(turned, 1)

                def project(u):
                    pe.wait_ge(kept, u // 2 + 1)
                    if u >= 2:
                        pe.wait_ge(v_kept, u - 1)
                    for t in range(TPU):
                        at = P * (TPU * u + t)
                        last = pe.matmul(PS[:, TPU * (u % 2) + t, 0:3 * D], XNV[:, at:at + P], WQKV[:, layer, :],
                                         start=True, stop=True)
                    last.then_inc(qkv_ready, 1)

                def stack(u):
                    pe.wait_ge(low, u + 1)
                    pe.wait_ge(doubled, u + 1)
                    pe.wait_ge(edge, min(4, 3 + u))
                    for f in range(4):
                        n = 4 * u + f
                        if n >= 3:
                            pe.wait_ge(stored, n - 2)
                        for k in range(4):
                            for t in range(TPU):
                                h = 8 * (f % 2) + 2 * k
                                last = pe.transpose(
                                    bank_bf(E_BANKS + n % 3)[:, (TPU * k + t) * P:(TPU * k + t + 1) * P],
                                    ASM[u % 2][:, f // 2, t, h:h + 2, :].rearrange("p h c -> p (h c)"), IDB[:, :])
                        last.then_inc(stacked, 1)

                pe.wait_ge(ident_ready, 3)
                turn(0)
                turn(1)
                pe.wait_ge(ld_qkv, 16)
                project(0)
                project(1)
                turn(2)
                project(2)
                project(3)
                turn(3)
                for u in range(NU):
                    if u == 0:
                        for n in range(4, NU):
                            project(n)
                    stack(u)
                    for t in BESIDE.get(u, ()):
                        lead(0, t)
                for t in BEHIND:
                    lead(0, t)
                pe.wait_ge(stored, 4 * NU)
                pe.wait_ge(m_kept, 2)
                drive(pe, step)
                for s in range(STEPS - LAG, STEPS):
                    product(NG - 1, s)
                pe.wait_ge(o_ready, NG * NB - 1)
                pe.wait_ge(m_kept, NG * NB)
                turn_output(NG - 1, NB - 1)

            def vector(dve):
                def reduce(g, t):
                    b, c, q, w = max_step(t)
                    if t == FIRST[b]:
                        wait_for(dve, nm_ready, g * NB + b)
                    for pair in range(2):
                        wait_for(dve, s_full, g * (2 * STEPS) + (2 * t + pair + 1))
                        dve.tensor_reduce(MX[:, c, q, 2 * pair:2 * pair + 2],
                                          PS[:, S_BANKS + 2 * pair:S_BANKS + 2 * pair + 2, 0:w], AX.X, ALU.max)\
                           .then_inc(s_read, 1)
                    if t in M_END:
                        wait_for(dve, s_read, g * (2 * STEPS) + 2 * (t + 1))
                        wait_for(dve, mp_ready, g * NB + b)
                        dve.tensor_reduce(NM[:, :], MX[:, 0:b + 1, :, :].rearrange("p c q j -> p (q j) c"),
                                          AX.X, ALU.max, negate=True).then_inc(nm_ready, 1)

                def keep_max(g, b):
                    wait_for(dve, m_turned, g * NB + (b + 1))
                    before = g * 64 + (64 if b >= 2 else 0)
                    wait_for(dve, m_written[(b - 2) % NB], before)
                    dve.tensor_copy(MT[:, b % 2, :], bank_bf(max_bank(g, b))[0:3 * HG, 0:BLK]).then_inc(m_kept, 1)

                def normalise(g, b):
                    wait_for(dve, o_turned, g * NB + (b + 1))
                    o = bank(out_bank(b)).rearrange("p (q j c) -> p q j c", q=TPB, j=HG)
                    dve.reciprocal(RD[:, :, :], o[:, :, :, DH]).then_inc(recip, 1)
                    wait_for(dve, recip, g * NB + (b + 1))
                    dst = ATT[:, TPB * b:TPB * (b + 1), bass.ds(g * (HG * DH), HG * DH)]
                    dve.tensor_tensor(dst.rearrange("p q (j d) -> p q j d", d=DH), o[:, :, :, 0:DH],
                                      RD[:, :, :].unsqueeze(3).broadcast_to([P, TPB, HG, DH]), ALU.mult)\
                       .then_inc(o_ready, 1)

                def lead(g, t):
                    reduce(g, t)
                    if t - M_TURN in M_END:
                        keep_max(g, M_END[t - M_TURN])

                def step(g, s, prev, nxt):
                    if at := beside(g, s, nxt):
                        reduce(*at)
                    if at := maxima_ended(g, s, nxt, M_TURN):
                        keep_max(*at)
                    if at := block_ended(g, s, prev, O_TURN):
                        normalise(*at)
                    if isinstance(g, int) and g == NG - 1 and s >= HEAD:
                        if layer == 0 and s == PREPARE:
                            prepare_weights(dve, Chain(dve, dve_chain))
                        if layer == 0 and s == max(TURN_WEIGHTS):
                            for n in range(len(TURNED)):
                                keep_weights(dve, n)
                        if s in PROJECT_ATT:
                            keep_attention(dve, layer, PROJECT_ATT[s])
                            add_attention(dve, link, layer, PROJECT_ATT[s])

                def rotate(u):
                    dve.wait_ge(qk_kept, u + 1)
                    x1, x2 = (QK[:, u].rearrange("p t a (m two) -> p t a m two", two=2)[:, :, :, :, n] for n in (0, 1))
                    y1, y2 = (ROT[u % 2].rearrange("p (a t m two) -> p t a m two", a=2, t=TPU, two=2)[:, :, :, :, n]
                              for n in (0, 1))
                    cos, sin = (v[:, layer, TPU * u:TPU * (u + 1), :].unsqueeze(2).broadcast_to([P, TPU, 2, D // 2])
                                for v in (COS, SIN))
                    if u >= 1:
                        dve.wait_ge(rotated, u)
                    dve.tensor_tensor(tmp[0], x1, cos, ALU.mult)
                    dve.tensor_tensor(tmp[1], x2, sin, ALU.mult)
                    dve.tensor_tensor(tmp[2], x1, sin, ALU.mult)
                    link(dve.tensor_tensor(tmp[3], x2, cos, ALU.mult))
                    dve.tensor_tensor(y1, tmp[0], tmp[1], ALU.subtract)
                    dve.tensor_tensor(y2, tmp[2], tmp[3], ALU.add).then_inc(rotated, 1)

                link = Chain(dve, chain)
                if layer == 0:
                    row_statistics(dve, link, range(NB), var_ready[0], ld_x)
                    invert_roots(dve, link, 1, range(NB), root_ready[0])
                    for b in range(NB):
                        normalise_rows(dve, b).then_inc(normed, 1)
                        if b == 0:
                            reduce_angles(dve, link, 0)
                else:
                    invert_roots(dve, link, 2, (NB - 1,), root_ready[2])
                    normalise_rows(dve, NB - 1).then_inc(normed, 1)
                if layer == 0:
                    cosines(dve, link, 0)
                dve.wait_ge(tables, layer + 1)
                rotate(0)
                for u in range(NU):
                    dve.wait_ge(high, u + 1)
                    if u >= 1:
                        dve.wait_ge(rest2, u)
                    dve.tensor_tensor(rows_of(R1), rows_of(ROT[u % 2]), asm_rows(u, 0), ALU.subtract).then_inc(rest1, 1)
                    if u + 1 < NU:
                        rotate(u + 1)
                    dve.wait_ge(mid, u + 1)
                    if u >= 1:
                        dve.wait_ge(low, u)
                    dve.tensor_tensor(rows_of(R2), rows_of(R1), asm_rows(u, 3), ALU.subtract).then_inc(rest2, 1)
                    for t in BESIDE.get(u - 1, ()):
                        lead(0, t)
                for t in (*BESIDE[NU - 1], *BEHIND):
                    lead(0, t)
                drive(dve, step)
                normalise(NG - 1, NB - 1)

            def scalar(act):
                def keep_output(g, b):
                    wait_for(act, pv_done, g * STEPS + FIRST[b + 1])
                    wait_for(act, o_turned, g * NB + b)
                    act.activation(OT[:, :], bank(O_BANK), ACT.Copy).then_inc(o_kept, 1)

                def step(g, s, prev, nxt):
                    b, kt, q0 = exp_step(s)
                    wait_for(act, pv_done, g * STEPS + (s - NSLOT // HG + 1))
                    for j in range(HG):
                        e = 4 * s + j
                        wait_for(act, e_full, g * (4 * STEPS) + (e + 1))
                        act.activation(PR[:, e % NSLOT, 0:BLK - q0], PS[:, turning_bank(s, "exp", j), 0:BLK - q0],
                                       ACT.Exp, scale=SCALE).then_inc(e_done, 1)
                        if j == 1 and (at := block_ended(g, s, prev, O_KEEP)):
                            keep_output(*at)

                def keep_turned(b):
                    act.wait_ge(turned, b + 1)
                    act.activation(XNV[:, BLK * b:BLK * (b + 1)], bank(O_BANK + b % 2), ACT.Copy).then_inc(kept, 1)

                def keep_qkv(u):
                    act.wait_ge(qkv_ready, u + 1)
                    banks = slice(TPU * (u % 2), TPU * (u % 2) + TPU)
                    act.activation(QK[:, u].rearrange("p t a n -> p t (a n)"), PS[:, banks, 0:2 * D], ACT.Copy)\
                       .then_inc(qk_kept, 1)
                    act.activation(VX[:, TPU * u:TPU * (u + 1), :, 0:DH],
                                   PS[:, banks, 2 * D:3 * D].rearrange("p t (h d) -> p t h d", d=DH), ACT.Copy)\
                       .then_inc(v_kept, 1)

                def store(n):
                    u, f = divmod(n, 4)
                    act.wait_ge(stacked, n + 1)
                    dst = (QA, KA)[f // 2][:, 4 * (f % 2):4 * (f % 2) + 4, TPU * P * u:TPU * P * (u + 1)].bitcast(I32)
                    act.copy(dst, PS[:, E_BANKS + n % 3, :].bitcast(I32).rearrange("p (s n) -> p s n", s=4))\
                       .then_inc(stored, 1)

                def write_high(u):
                    act.wait_ge(rotated, u + 1)
                    if u >= 2:
                        act.wait_ge(stacked, 4 * (u - 1))
                    act.activation(asm_rows(u, 0), rows_of(ROT[u % 2]), ACT.Copy).then_inc(high, 1)

                if layer == 0:
                    load_biases(act)
                    root(act, 1, range(NB), var_ready[0], root_ready[0])
                keep_turned(0)
                if layer == 0:
                    sines(act, 0)
                keep_turned(1)
                if layer == 1:
                    root(act, NB, (NB - 1,), var_ready[2], root_ready[2])
                keep_qkv(0)
                keep_qkv(1)
                keep_turned(2)
                keep_qkv(2)
                write_high(0)
                keep_qkv(3)
                keep_turned(3)
                for u in range(NU):
                    if u >= 1:
                        store(4 * (u - 1))
                        store(4 * (u - 1) + 1)
                    if 2 * u + 5 < NU:
                        keep_qkv(2 * u + 4)
                    act.wait_ge(rest1, u + 1)
                    act.activation(asm_rows(u, 3), rows_of(R1), ACT.Copy).then_inc(mid, 1)
                    if u >= 1:
                        store(4 * (u - 1) + 2)
                        store(4 * (u - 1) + 3)
                    if 2 * u + 5 < NU:
                        keep_qkv(2 * u + 5)
                    if u + 1 < NU:
                        write_high(u + 1)
                    act.wait_ge(rest2, u + 1)
                    half = TPU * H
                    act.activation(part(u, 0, 5), rows_of(R2)[:, 0:half, :], ACT.Copy)
                    act.activation(part(u, 1, 4), rows_of(R2)[:, half:, :], ACT.Copy).then_inc(low, 1)
                for f in range(4):
                    store(4 * (NU - 1) + f)
                drive(act, step)
                keep_output(NG - 1, NB - 1)

            def gpsimd(pool):
                def load_v(g, b):
                    tiles = slice(TPB * b, TPB * (b + 1))
                    pool.tensor_copy(VG[:, tiles, :, 0:DH + 1], VX[:, tiles, bass.ds(g * HG, HG), :]).then_inc(v_loaded, 1)

                def split_max(g, b):
                    wait_for(pool, nm_ready, g * NB + (b + 1))
                    wait_for(pool, m_turned, g * NB + b)
                    mp = MP[:, :, :, :].rearrange("p q j n -> p (q j) n")
                    pool.tensor_copy(mp[:, :, 0], NM[:, :]).then_inc(nm_chain, 1)
                    wait_for(pool, nm_chain, g * (4 * NB) + (4 * b + 1))
                    pool.tensor_tensor(NR[:, 0, :], NM[:, :], mp[:, :, 0], ALU.subtract).then_inc(nm_chain, 1)
                    wait_for(pool, nm_chain, g * (4 * NB) + (4 * b + 2))
                    pool.tensor_copy(mp[:, :, 1], NR[:, 0, :]).then_inc(nm_chain, 1)
                    wait_for(pool, nm_chain, g * (4 * NB) + (4 * b + 3))
                    pool.tensor_tensor(NR[:, 1, :], NR[:, 0, :], mp[:, :, 1], ALU.subtract).then_inc(nm_chain, 1)
                    wait_for(pool, nm_chain, g * (4 * NB) + (4 * b + 4))
                    pool.tensor_copy(mp[:, :, 2], NR[:, 1, :]).then_inc(mp_ready, 1)

                def lead(g, t):
                    if t in M_END:
                        split_max(g, M_END[t])

                def step(g, s, prev, nxt):
                    b, kt, q0 = exp_step(s)
                    n = s - LAG - 1 - FIRST[NB - 1]
                    if n > 0 and n % TPB == 0 and nxt is not None:
                        wait_for(pool, pv_done, g * STEPS + (s - LAG - 1))
                        load_v(nxt, n // TPB - 1)
                    if s == LAG and prev is not None:
                        wait_for(pool, pv_done, g * STEPS)
                        load_v(g, NB - 1)
                    if kt >= TPB * b:
                        wait_for(pool, e_done, g * (4 * STEPS) + 4 * (s + 1))
                        v = PR[:, 4 * s % NSLOT:4 * s % NSLOT + HG, 0:P]
                        pool.affine_select(out=v, in_=v, compare_op=ALU.is_ge, fill=0.0, base=0,
                                           pattern=[[0, HG], [1, P]], channel_multiplier=-1).then_inc(masked, 1)
                    if at := maxima_ended(g, s, nxt, 0):
                        split_max(*at)

                if layer == 1:
                    last = Chain(pool, sem("l1_angle_chain"))
                    pool.wait_ge(raw_ready, 1)
                    angles(pool, last, 1)
                    cosines(pool, last, 1)
                    pool.wait_ge(normed, 1)
                if layer == 0:
                    constants(pool)
                    first = Chain(pool, pool_chain)
                    first.n = 4
                    angles(pool, first, 0)
                for n in range(2):
                    pool.memset(ASM[n].bitcast(I32)[:, :, :, :, MROW // 2:ROWS // 2], 0).then_inc(edge, 1)
                for n in range(2):
                    pool.wait_ge(edge, n + 1)
                    pool.memset(ASM[n][:, 1, :, :, MROW:MROW + 3], 1.0).then_inc(edge, 1)
                if layer == 0:
                    pool.memset(K2[:, :, :].bitcast(I32), 0).then_inc(zeroed, 1)
                    pool.memset(VX[:, :, :, DH:DH + 1], 1.0).then_inc(zeroed, 1)
                for u in range(NU):
                    pool.wait_ge(high, u + 1)
                    for a, to in ((0, slice(1, 5, 3)), (1, slice(2, 6, 3))):
                        v = words(u, a)
                        pool.tensor_copy(v[:, :, to, :], v[:, :, 0:1, :].broadcast_to([P, TPU * H, 2, DH // 2]))
                    pool.wait_ge(mid, u + 1)
                    for a, to in ((0, 2), (1, 1)):
                        v = words(u, a)
                        last = pool.tensor_copy(v[:, :, to, :], v[:, :, 3, :])
                    last.then_inc(doubled, 1)
                    for t in BESIDE.get(u - 1, ()):
                        lead(0, t)
                pool.wait_ge(v_kept, NU)
                pool.wait_ge(qkv_ready, NU)
                pool.memset(VG[:, :, :, :], 0.0).then_inc(zeroed, 1)
                pool.wait_ge(zeroed, 3 + layer)
                for b in range(NB):
                    load_v(0, b)
                for t in (*BESIDE[NU - 1], *BEHIND):
                    lead(0, t)
                drive(pool, step)

            return Programs(sync, tensor, vector, scalar, gpsimd)

        AT = work(8704, T)

        def turn_attention(pe, layer, b):
            pe.wait_ge(normalised[layer], (NG - 1) * NB + b + 1)
            for t in range(TPB):
                last = pe.transpose(PS[:, AT_BANKS[b], t * P:(t + 1) * P], ATT[:, TPB * b + t, :], IDF[:, :])
            last.then_inc(a_turned[layer], 1)

        def keep_attention(dve, layer, b):
            dve.wait_ge(a_turned[layer], b + 1)
            dve.tensor_copy(AT[:, BLK * b:BLK * (b + 1)], bank(AT_BANKS[b])).then_inc(a_kept[layer], 1)

        def project_attention(pe, layer, b):
            pe.wait_ge(a_kept[layer], b + 1)
            if 1 <= b < NB - 1:
                pe.wait_ge(added[layer], b)
            for t in range(TPB):
                at = P * (TPB * b + t)
                last = pe.matmul(PS[:, WO_BANKS[b], t * P:(t + 1) * P], AT[:, at:at + P], WO[:, layer, :],
                                 start=True, stop=True)
            last.then_inc(projected[layer], 1)

        def add_attention(dve, link, layer, b):
            dve.wait_ge(projected[layer], b + 1)
            x = X[:, TPB * b:TPB * (b + 1), :].rearrange("p t d -> p (t d)")
            dve.tensor_tensor(x, x, bank(WO_BANKS[b]), ALU.add).then_inc(added[layer], 1)
            dve.wait_ge(added[layer], b + 1)
            row_statistics(dve, link, (b,), var_ready[2 * layer + 1])

        def feed_forward(layer):
            L = f"l{layer}_"
            normed, turned, kept = sem(L + "ff_normed"), sem(L + "ff_turned"), sem(L + "ff_kept")
            hid_full, hid_done, gate_done = sem(L + "hid_full"), sem(L + "hid_done"), sem(L + "gate_done")
            down, chain, stored = sem(L + "down"), sem(L + "ff_chain"), sem(L + "stored")
            x_done = sem(L + "x_done")
            ln = 2 * layer + 1
            nh = (C0, C1)[layer]
            XNT = VG[:, :, :, :].rearrange("p i j c -> p (i j c)")
            HT = [work(2048 + 512 * n, 512) for n in range(2 * nh)]
            GT = [work(6144 + 512 * n, 512) for n in range(2)]

            def tensor(pe):
                def turn(b):
                    pe.wait_ge(normed, b + 1)
                    if b >= 2:
                        pe.wait_ge(kept, b - 1)
                    for t in range(TPB):
                        last = pe.transpose(PS[:, O_BANK + b % 2, t * P:(t + 1) * P], XN[:, TPB * b + t, :], IDF[:, :])
                    last.then_inc(turned, 1)

                def up(b):
                    pe.wait_ge(kept, b + 1)
                    if b == 0:
                        pe.wait_ge(added[layer], NB - 1)
                    xs = XNT[:, BLK * b:BLK * (b + 1)]
                    for c in range(nh):
                        for k, w in enumerate((W1T,) if layer == 0 else (WGT, WUT)):
                            n = ((1, 2)[layer]) * (nh * b + c) + k
                            if n >= 4:
                                pe.wait_ge(hid_done if layer == 0 or k else gate_done,
                                           n - 3 if layer == 0 else (n - 4) // 2 + 1)
                            pe.matmul(bank(n % 4), w[:, c * P:(c + 1) * P], xs, start=True, stop=True).then_inc(hid_full, 1)

                def back(b):
                    pe.wait_ge(hid_done, nh * (b + 1))
                    pe.wait_ge(added[layer], NB)
                    if b >= 2:
                        pe.wait_ge(x_done, b - 1)
                    w = (W2T, WDT)[layer]
                    for t in range(TPB):
                        for c in range(nh):
                            last = pe.matmul(PS[:, E_BANKS + b % 2, t * P:(t + 1) * P],
                                             HT[nh * (b % 2) + c][:, t * P:(t + 1) * P], w[:, c, :],
                                             start=(c == 0), stop=(c == nh - 1))
                    last.then_inc(down, 1)

                turn_attention(pe, layer, NB - 1)
                turn(0)
                project_attention(pe, layer, NB - 1)
                for b in range(NB):
                    if b + 1 < NB:
                        turn(b + 1)
                    up(b)
                    if b >= 1:
                        back(b - 1)
                back(NB - 1)

            def scalar(act):
                root(act, NB - 1, range(NB - 1), var_ready[ln], root_ready[ln])
                for b in range(NB):
                    act.wait_ge(turned, b + 1)
                    act.activation(XNT[:, BLK * b:BLK * (b + 1)], bank(O_BANK + b % 2), ACT.Copy).then_inc(kept, 1)
                    if b == 0:
                        root(act, NB, (NB - 1,), var_ready[ln], root_ready[ln])
                        if layer == 0:
                            act.wait_ge(ld_b, 48)
                    for c in range(nh):
                        n = nh * b + c
                        if layer == 0:
                            act.wait_ge(hid_full, n + 1)
                            if b >= 2:
                                act.wait_ge(down, b - 1)
                            act.activation(HT[nh * (b % 2) + c], bank(n % 4), ACT.Gelu, bias=B1[:, c:c + 1])\
                               .then_inc(hid_done, 1)
                        else:
                            act.wait_ge(hid_full, 2 * n + 1)
                            if n >= 2:
                                act.wait_ge(hid_done, n - 1)
                            act.activation(GT[n % 2], bank(2 * n % 4), ACT.Silu).then_inc(gate_done, 1)
                if layer == 0:
                    sines(act, 1)
                    root(act, NB - 1, range(NB - 1), var_ready[2], root_ready[2])

            def vector(dve):
                link = Chain(dve, chain)

                def add(b):
                    dve.wait_ge(down, b + 1)
                    x = X[:, TPB * b:TPB * (b + 1), :]
                    o = bank(E_BANKS + b % 2).rearrange("p (t d) -> p t d", t=TPB)
                    if layer == 0:
                        tmp = XN[:, TPB * b:TPB * (b + 1), :]
                        link(dve.tensor_tensor(tmp, o, B2[:, :].unsqueeze(1).broadcast_to([P, TPB, D]), ALU.add))
                        dve.tensor_tensor(x, x, tmp, ALU.add).then_inc(x_done, 1)
                        dve.wait_ge(x_done, b + 1)
                        row_statistics(dve, link, (b,), var_ready[2])
                    else:
                        dve.tensor_tensor(x, x, o, ALU.add).then_inc(x_done, 1)

                invert_roots(dve, link, 1, range(NB - 1), root_ready[ln])
                normalise_rows(dve, 0).then_inc(normed, 1)
                keep_attention(dve, layer, NB - 1)
                for b in range(1, NB - 1):
                    normalise_rows(dve, b).then_inc(normed, 1)
                add_attention(dve, link, layer, NB - 1)
                invert_roots(dve, link, 2, (NB - 1,), root_ready[ln])
                normalise_rows(dve, NB - 1).then_inc(normed, 1)
                if layer == 0:
                    reduce_angles(dve, link, 1)
                    dve.wait_ge(ld_b, 48)
                for b in range(NB):
                    if layer == 1:
                        for c in range(nh):
                            n = nh * b + c
                            dve.wait_ge(gate_done, n + 1)
                            dve.wait_ge(hid_full, 2 * n + 2)
                            if b >= 2:
                                dve.wait_ge(down, b - 1)
                            dve.tensor_tensor(HT[nh * (b % 2) + c], GT[n % 2], bank((2 * n + 1) % 4), ALU.mult)\
                               .then_inc(hid_done, 1)
                        if b >= 1:
                            add(b - 1)
                    else:
                        if b == NB - 1:
                            invert_roots(dve, link, 1, range(NB - 1), root_ready[2])
                            for n in range(NB - 1):
                                normalise_rows(dve, n).then_inc(att_normed[1], 1)
                        add(b)
                if layer == 1:
                    add(NB - 1)

            def sync(sp):
                if layer == 1:
                    for b in range(NB):
                        sp.wait_ge(x_done, b + 1)
                        sp.dma_start(out[0, BLK * b:BLK * (b + 1), :].rearrange("(i p) d -> p i d", p=P),
                                     X[:, TPB * b:TPB * (b + 1), :]).then_inc(stored, 16)
                    sp.wait_ge(stored, 16 * NB)

            return Programs(sync, tensor, vector, scalar)

        att0, ff0, att1, ff1 = attention(0), feed_forward(0), attention(1), feed_forward(1)

        with nc.Block() as block:
            @block.sync
            def _(sp):
                att0.sync(sp)
                att1.sync(sp)
                ff1.sync(sp)

            @block.tensor
            def _(pe):
                for part in (att0, ff0, att1, ff1):
                    part.tensor(pe)

            @block.vector
            def _(dve):
                for part in (att0, ff0, att1, ff1):
                    part.vector(dve)

            @block.scalar
            def _(act):
                for part in (att0, ff0, att1, ff1):
                    part.scalar(act)

            @block.gpsimd
            def _(pool):
                att0.gpsimd(pool)
                att1.gpsimd(pool)


_INS = ['L0_attn_x', 'L0_attn_w_qkv', 'L0_attn_w_o', 'L0_attn_log_scale', 'L0_ffn_w1', 'L0_ffn_b1', 'L0_ffn_w2',
        'L0_ffn_b2', 'L1_attn_W_q', 'L1_attn_W_k', 'L1_attn_W_v', 'L1_attn_W_o', 'L1_ffn_w_gate', 'L1_ffn_w_up',
        'L1_ffn_w_down']


def kernel(**inputs):
    import numpy as _np
    import concourse.bacc as _bacc
    from concourse import mybir as _mybir
    from concourse.bass_utils import run_bass_kernel_spmd as _run

    nc = _bacc.Bacc("TRN2", target_bir_lowering=False, num_devices=1)
    arrays, args = {}, []
    for name in _INS:
        a = _np.ascontiguousarray(inputs[name])
        arrays[f"in_{name}"] = a
        args.append(nc.dram_tensor(f"in_{name}", a.shape, _mybir.dt.from_np(a.dtype), kind="ExternalInput").ap())
    args.append(nc.dram_tensor("out_x", (1, T, D), _mybir.dt.float32, kind="ExternalOutput").ap())
    build(nc, *args)
    r = _run(nc, [arrays], core_ids=[0])
    return r.results[0]["out_x"]
```
